# Optimizing a Trainium2 kernel written in Bass

```python
import numpy as np
import jax
import jax.numpy as jnp

def _softmax(x, axis=-1):
    return jax.nn.softmax(x, axis=axis)

def _gelu(x):
    return jax.nn.gelu(x, approximate=True)

def _silu(x):
    return jax.nn.silu(x)

def _sigmoid(x):
    return jax.nn.sigmoid(x)

def _layernorm(x, axis=-1, eps=1e-05):
    m = jnp.mean(x, axis=axis, keepdims=True)
    v = jnp.var(x, axis=axis, keepdims=True)
    return (x - m) / jnp.sqrt(v + eps)

def _scatter_add(tgt, idx, src, axis=0):
    return tgt.at[idx].add(src)

def _segment_sum(src, seg, n):
    return jax.ops.segment_sum(src, seg, n)
kernel_name = 'mk_xattn_seq_d2_seqx_r2_2a613f'

def setup_inputs(seed: int=0):
    np.random.seed(seed)
    _w = jnp.asarray

    def _rec_inputs():
        import jax
        import jax.numpy as jnp
        _rk = jax.random.key(seed)
        x = 7.22e-05 + 1 * jax.random.normal(jax.random.fold_in(_rk, 1), (2, 2048, 512), jnp.float32)
        _lenS = 2048 - jax.random.randint(jax.random.fold_in(_rk, 7), (2,), 0, max(1, 2048 // 4) + 1, jnp.int32)
        _lenS2 = 77 - jax.random.randint(jax.random.fold_in(_rk, 8), (2,), 0, max(1, 77 // 4) + 1, jnp.int32)
        _ctx_1024P = jax.random.normal(jax.random.fold_in(_rk, 11), (2, 16, 512), jnp.float32)
        _ctx_1024c = jax.random.dirichlet(jax.random.fold_in(_rk, 511), 0.3 * jnp.ones((16,), jnp.float32), (2, 77))
        _ctx_1024t = jnp.einsum('bsk,bkd->bsd', _ctx_1024c, _ctx_1024P)
        _ctx_1024t = _ctx_1024t * jax.lax.rsqrt(jnp.mean(jnp.square(_ctx_1024t)) + 1e-12) * 0.953939
        ctx_1024 = 4.13588e-05 + 0.999923 * (_ctx_1024t + 0.3 * jax.random.normal(jax.random.fold_in(_rk, 611), (2, 77, 512), jnp.float32))
        _validS = jnp.arange(2048)[None, :] < _lenS[:, None]
        _validS2 = jnp.arange(77)[None, :] < _lenS2[:, None]
        _causal = jnp.tril(jnp.ones((2048, 2048), dtype=bool))
        mask_BxSxS2_ik0 = jnp.where(jnp.broadcast_to(_validS2[:, None, :], (2, 2048, 77)), 0, 1).astype(jnp.int32)
        return (x, ctx_1024, mask_BxSxS2_ik0)
    x, ctx_1024, mask_BxSxS2_ik0 = _rec_inputs()

    def _L0_xattn_setup():
        import jax, jax.numpy as jnp
        import numpy as np
        D = 512
        B, SX, SY = (4, 1024, 1024)
        NEG = -1000000000.0
        key = jax.random.key(seed)
        ks = jax.random.split(key, 9)
        s = 1.0 / np.sqrt(D)
        return {'x': jax.random.normal(ks[0], (B, SX, D), jnp.float32), 'y': jax.random.normal(ks[1], (B, SY, D), jnp.float32), 'mask': jax.random.randint(ks[2], (B, SX, SY), 0, 2, jnp.int32), 'Wq': jax.random.uniform(ks[3], (D, D), jnp.float32, -s, s), 'bq': jax.random.uniform(ks[4], (D,), jnp.float32, -s, s), 'Wk': jax.random.uniform(ks[5], (D, D), jnp.float32, -s, s), 'bk': jax.random.uniform(ks[6], (D,), jnp.float32, -s, s), 'Wv': jax.random.uniform(ks[7], (D, D), jnp.float32, -s, s), 'bv': jax.random.uniform(ks[8], (D,), jnp.float32, -s, s)}
    _L0_xattn_all = _L0_xattn_setup()
    _L0_xattn_in = {k: v for k, v in _L0_xattn_all.items() if k in ('Wq', 'bq', 'Wk', 'bk', 'Wv', 'bv')}
    del _L0_xattn_all

    def _L1_xattn_setup():
        import jax, jax.numpy as jnp
        import numpy as np
        D_MODEL = 512
        N_HEADS = 16
        D_K = D_MODEL // N_HEADS
        LN_EPS = 1e-05

        def _attention(query, key_value, W_qkv, b_qkv, W_o, b_o, ln_gamma, ln_beta):
            B, Sq, _ = query.shape
            Skv = key_value.shape[1]
            Wq, Wk, Wv = (W_qkv[:D_MODEL], W_qkv[D_MODEL:2 * D_MODEL], W_qkv[2 * D_MODEL:])
            bq, bk, bv = (b_qkv[:D_MODEL], b_qkv[D_MODEL:2 * D_MODEL], b_qkv[2 * D_MODEL:])
            Q = (query @ Wq.T + bq).reshape(B, Sq, N_HEADS, D_K).transpose(0, 2, 1, 3)
            K = (key_value @ Wk.T + bk).reshape(B, Skv, N_HEADS, D_K).transpose(0, 2, 1, 3)
            V = (key_value @ Wv.T + bv).reshape(B, Skv, N_HEADS, D_K).transpose(0, 2, 1, 3)
            scores = jnp.einsum('bhqd,bhkd->bhqk', Q.astype(jnp.float32), K.astype(jnp.float32))
            scores = scores / np.sqrt(D_K)
            attn = jax.nn.softmax(scores, axis=-1)
            context = jnp.einsum('bhqk,bhkd->bhqd', attn, V.astype(jnp.float32)).astype(query.dtype)
            context = context.transpose(0, 2, 1, 3).reshape(B, Sq, D_MODEL)
            output = context @ W_o.T + b_o
            x = output + query
            mu = jnp.mean(x, axis=-1, keepdims=True)
            var = jnp.mean(jnp.square(x - mu), axis=-1, keepdims=True)
            return (x - mu) / jnp.sqrt(var + LN_EPS) * ln_gamma + ln_beta
        key = jax.random.key(seed)
        ks = jax.random.split(key, 8)
        B, Sq, Skv = (2, 1024, 1024)
        scale = 1.0 / np.sqrt(D_MODEL)
        return {'query': jax.random.normal(ks[0], (B, Sq, D_MODEL), dtype=jnp.float32), 'key_value': jax.random.normal(ks[1], (B, Skv, D_MODEL), dtype=jnp.float32), 'W_qkv': jax.random.normal(ks[2], (3 * D_MODEL, D_MODEL), dtype=jnp.float32) * scale, 'b_qkv': jax.random.normal(ks[3], (3 * D_MODEL,), dtype=jnp.float32) * 0.01, 'W_o': jax.random.normal(ks[4], (D_MODEL, D_MODEL), dtype=jnp.float32) * scale, 'b_o': jax.random.normal(ks[5], (D_MODEL,), dtype=jnp.float32) * 0.01, 'ln_gamma': jnp.ones((D_MODEL,), dtype=jnp.float32), 'ln_beta': jnp.zeros((D_MODEL,), dtype=jnp.float32)}
    _L1_xattn_all = _L1_xattn_setup()
    _L1_xattn_in = {k: v for k, v in _L1_xattn_all.items() if k in ('W_qkv', 'b_qkv', 'W_o', 'b_o', 'ln_gamma', 'ln_beta')}
    del _L1_xattn_all
    return {'x': x, 'ctx_1024': ctx_1024, 'mask_BxSxS2_ik0': mask_BxSxS2_ik0, 'L0_xattn_Wq': _L0_xattn_in['Wq'], 'L0_xattn_bq': _L0_xattn_in['bq'], 'L0_xattn_Wk': _L0_xattn_in['Wk'], 'L0_xattn_bk': _L0_xattn_in['bk'], 'L0_xattn_Wv': _L0_xattn_in['Wv'], 'L0_xattn_bv': _L0_xattn_in['bv'], 'L1_xattn_W_qkv': _L1_xattn_in['W_qkv'], 'L1_xattn_b_qkv': _L1_xattn_in['b_qkv'], 'L1_xattn_W_o': _L1_xattn_in['W_o'], 'L1_xattn_b_o': _L1_xattn_in['b_o'], 'L1_xattn_ln_gamma': _L1_xattn_in['ln_gamma'], 'L1_xattn_ln_beta': _L1_xattn_in['ln_beta']}

def reference(x, ctx_1024, mask_BxSxS2_ik0, L0_xattn_Wq, L0_xattn_bq, L0_xattn_Wk, L0_xattn_bk, L0_xattn_Wv, L0_xattn_bv, L1_xattn_W_qkv, L1_xattn_b_qkv, L1_xattn_W_o, L1_xattn_b_o, L1_xattn_ln_gamma, L1_xattn_ln_beta):
    import jax
    import jax.numpy as jnp

    def _L0_xattn_ref(x, y, mask, Wq, bq, Wk, bk, Wv, bv):
        import jax, jax.numpy as jnp
        import numpy as np
        D = 512
        B, SX, SY = (4, 1024, 1024)
        NEG = -1000000000.0
        q = jnp.einsum('bsd,ed->bse', x, Wq) + bq
        k = jnp.einsum('btd,ed->bte', y, Wk) + bk
        v = jnp.einsum('btd,ed->bte', y, Wv) + bv
        scores = jnp.einsum('bsd,btd->bst', q, k)
        scores = jnp.where(mask == 0, NEG, scores)
        attn = jax.nn.softmax(scores, axis=-1)
        out = jnp.einsum('bst,btd->bsd', attn, v)
        return out + x

    def _L1_xattn_ref(query, key_value, W_qkv, b_qkv, W_o, b_o, ln_gamma, ln_beta):
        import jax, jax.numpy as jnp
        import numpy as np
        D_MODEL = 512
        N_HEADS = 16
        D_K = D_MODEL // N_HEADS
        LN_EPS = 1e-05

        def _attention(query, key_value, W_qkv, b_qkv, W_o, b_o, ln_gamma, ln_beta):
            B, Sq, _ = query.shape
            Skv = key_value.shape[1]
            Wq, Wk, Wv = (W_qkv[:D_MODEL], W_qkv[D_MODEL:2 * D_MODEL], W_qkv[2 * D_MODEL:])
            bq, bk, bv = (b_qkv[:D_MODEL], b_qkv[D_MODEL:2 * D_MODEL], b_qkv[2 * D_MODEL:])
            Q = (query @ Wq.T + bq).reshape(B, Sq, N_HEADS, D_K).transpose(0, 2, 1, 3)
            K = (key_value @ Wk.T + bk).reshape(B, Skv, N_HEADS, D_K).transpose(0, 2, 1, 3)
            V = (key_value @ Wv.T + bv).reshape(B, Skv, N_HEADS, D_K).transpose(0, 2, 1, 3)
            scores = jnp.einsum('bhqd,bhkd->bhqk', Q.astype(jnp.float32), K.astype(jnp.float32))
            scores = scores / np.sqrt(D_K)
            attn = jax.nn.softmax(scores, axis=-1)
            context = jnp.einsum('bhqk,bhkd->bhqd', attn, V.astype(jnp.float32)).astype(query.dtype)
            context = context.transpose(0, 2, 1, 3).reshape(B, Sq, D_MODEL)
            output = context @ W_o.T + b_o
            x = output + query
            mu = jnp.mean(x, axis=-1, keepdims=True)
            var = jnp.mean(jnp.square(x - mu), axis=-1, keepdims=True)
            return (x - mu) / jnp.sqrt(var + LN_EPS) * ln_gamma + ln_beta
        return _attention(query, key_value, W_qkv, b_qkv, W_o, b_o, ln_gamma, ln_beta)
    x = _L0_xattn_ref(x, ctx_1024, mask_BxSxS2_ik0, L0_xattn_Wq, L0_xattn_bq, L0_xattn_Wk, L0_xattn_bk, L0_xattn_Wv, L0_xattn_bv)
    x = _L1_xattn_ref(x, ctx_1024, L1_xattn_W_qkv, L1_xattn_b_qkv, L1_xattn_W_o, L1_xattn_b_o, L1_xattn_ln_gamma, L1_xattn_ln_beta)
    return x

_drawn_inputs = setup_inputs


def setup_inputs(seed=0):
    import zlib

    import numpy as np

    out = dict(_drawn_inputs(seed))
    spreads = {'L1_xattn_ln_gamma': (1.0, 0.2), 'L1_xattn_ln_beta': (0.0, 0.1)}
    factors = {'L0_xattn_bk': 8.0, 'L0_xattn_bv': 2.798, 'L1_xattn_b_qkv': 7.411, 'L1_xattn_b_o': 7.162}
    for name, (base, spread) in spreads.items():
        noise = np.random.default_rng([zlib.crc32(name.encode()), seed]).standard_normal(out[name].shape)
        drawn = base * np.exp(spread * noise) if base else spread * noise
        out[name] = jnp.asarray(drawn.astype(out[name].dtype))
    for name, factor in factors.items():
        out[name] = (out[name] * factor).astype(out[name].dtype)
    return out
```

```python
from contextlib import ExitStack

import concourse.bass as bass
from concourse import mybir

F32 = mybir.dt.float32
F32R = mybir.dt.float32r
I32 = mybir.dt.int32
ALU = mybir.AluOpType
ACT = mybir.ActivationFunctionType
AX_X = mybir.AxisListType.X

BATCH, SEQ, DIM, KEYS = 2, 2048, 512, 77
HEADS = 16
HEAD_DIM = DIM // HEADS
P = 128
CH = DIM // P
GROUP_HEADS = P // HEAD_DIM
TILES = 4
BLOCK = TILES * P
BLOCKS = BATCH * SEQ // BLOCK
UNITS = BLOCKS * CH
GCOLS = GROUP_HEADS * KEYS
KC = 3
KROWS = -(-GCOLS // KC)
KSTART = [min(c * KROWS, GCOLS - KROWS) for c in range(KC)]
NEG = -1000000000.0
LN_EPS = 1e-05
SCALE = 1.0 / float(HEAD_DIM) ** 0.5
FIRST = 4
TURN = 2 * CH
TURNS = 3
LOOP_END = FIRST + TURN * TURNS
STEPS = UNITS + 4


def xattn_kernel(nc, xT, x, mask, ctxT, w0k, w0q, w0v, w1q, w1k, w1v, w1o, cols, rows, out):
    with ExitStack() as ctx:
        def sb(name, shape, dt=F32, stack=ctx):
            return stack.enter_context(nc.sbuf_tensor(name, shape, dt))

        def sem(name):
            return ctx.enter_context(nc.semaphore(name))

        with ExitStack() as prep:
            raw0 = sb("raw0", [P, CH, DIM], F32, prep)
            raw1 = sb("raw1", [P, CH, DIM], F32, prep)
            raw2 = sb("raw2", [P, CH, DIM], F32, prep)
            raw3 = sb("raw3", [P, CH, DIM], F32, prep)
            v1_h = sb("v1_h", [KEYS, BATCH, DIM], F32R, prep)
            v1_l = sb("v1_l", [KEYS, BATCH, DIM], F32R, prep)
            k0T = sb("k0T", [P, CH, BATCH * KEYS], F32, prep)
            v0T = sb("v0T", [P, CH, BATCH * KEYS], F32, prep)
            k1T = sb("k1T", [P, CH, BATCH * KEYS], F32, prep)
            v1T = sb("v1T", [P, CH, BATCH * KEYS], F32, prep)
            v0o = sb("v0o", [KEYS, BATCH, DIM], F32, prep)
        ct_h = sb("ct_h", [P, CH, BLOCK], F32R)
        ct_l = sb("ct_l", [P, CH, BLOCK], F32R)
        y = sb("y", [P, TILES, DIM])
        x_nat = sb("x_nat", [P, TILES, DIM])
        pt_h = sb("pt_h", [KROWS, KC, BLOCK], F32R)
        pt_l = sb("pt_l", [KROWS, KC, BLOCK], F32R)
        prob = sb("prob", [P, 2, TILES, GCOLS])

        wq_h = sb("wq_h", [P, CH, DIM], F32R)
        wq_l = sb("wq_l", [P, CH, DIM], F32R)
        wo_h = sb("wo_h", [P, CH, DIM], F32R)
        wo_l = sb("wo_l", [P, CH, DIM], F32R)
        a0 = sb("a0", [P, CH, BATCH * KEYS])
        c0 = sb("c0", [P, BATCH * KEYS])
        u_h = sb("u_h", [KEYS, BATCH, DIM], F32R)
        u_l = sb("u_l", [KEYS, BATCH, DIM], F32R)
        v0_h = sb("v0_h", [KEYS, BATCH, DIM], F32R)
        v0_l = sb("v0_l", [KEYS, BATCH, DIM], F32R)
        kd_h = sb("kd_h", [P, BATCH, CH, GCOLS], F32R)
        kd_l = sb("kd_l", [P, BATCH, CH, GCOLS], F32R)
        vd_h = sb("vd_h", [KROWS, BATCH, CH, KC, P], F32R)
        vd_l = sb("vd_l", [KROWS, BATCH, CH, KC, P], F32R)
        ctxT_sb = sb("ctxT_sb", [P, CH, BATCH * KEYS])
        cols_sb = sb("cols_sb", [P, 6, CH])
        rows_sb = sb("rows_sb", [P, 3, DIM])
        bq0_wide = sb("bq0_wide", [P, CH, P])
        ident = sb("ident", [P, P])
        minus_half = sb("minus_half", [P, TILES])

        x_raw = sb("x_raw", [P, CH, BLOCK])
        x_h = sb("x_h", [P, CH, BLOCK], F32R)
        x_l = sb("x_l", [P, CH, BLOCK], F32R)
        mask_sb = sb("mask_sb", [P, TILES, KEYS], I32)
        s0 = sb("s0", [P, TILES, KEYS])
        n0 = sb("n0", [P, TILES, KEYS])
        m0 = sb("m0", [P, TILES, KEYS])
        e0 = sb("e0", [P, TILES, KEYS])
        stat0 = sb("stat0", [P, 3, TILES])
        p0_h = sb("p0_h", [KEYS, 2, BLOCK], F32R)
        p0_l = sb("p0_l", [KEYS, 2, BLOCK], F32R)
        q_h = sb("q_h", [P, 2, BLOCK], F32R)
        q_l = sb("q_l", [P, 2, BLOCK], F32R)
        mx = sb("mx", [P, 2, TILES, GROUP_HEADS])
        sm = sb("sm", [P, 2, TILES, GROUP_HEADS])
        rc = sb("rc", [P, 2, TILES, GROUP_HEADS])
        bn6 = sb("bn6", [P, TILES, 6])
        both = sb("both", [P, TILES, 3])
        diff = sb("diff", [P, TILES])
        within = sb("within", [P, TILES])
        between = sb("between", [P, TILES])
        ve = sb("ve", [P, TILES])
        rs = sb("rs", [P, TILES])
        nb = sb("nb", [P, TILES])

        bank = [ctx.enter_context(nc.psum_tensor(f"bank{n}", [P, 512], F32)) for n in range(8)]
        ps_q, ps_s, ps_t, ps_pv, ps_out, ps_0 = bank[0], bank[1:3], bank[3:5], bank[5], bank[6], bank[7]

        ld_ctx, ld_cols, ld_rows = sem("ld_ctx"), sem("ld_cols"), sem("ld_rows")
        ld_w0k, ld_w0q, ld_w0v, ld_w1q = sem("ld_w0k"), sem("ld_w0q"), sem("ld_w0v"), sem("ld_w1q")
        ld_w1k, ld_w1v, ld_w1o = sem("ld_w1k"), sem("ld_w1v"), sem("ld_w1o")
        ld_xT, ld_mask, ld_x = sem("ld_xT"), sem("ld_mask"), sem("ld_x")
        vd_placed = sem("vd_placed")
        stored = [sem(f"stored{t}") for t in range(TILES)]
        mm_k0T, mm_a0, mm_c0, mm_v0T = sem("mm_k0T"), sem("mm_a0"), sem("mm_c0"), sem("mm_v0T")
        mm_v0, mm_u, mm_k1T, mm_v1T, mm_v1 = sem("mm_v0"), sem("mm_u"), sem("mm_k1T"), sem("mm_v1T"), sem("mm_v1")
        k0T_ready, v0T_ready, k1T_ready, v1T_ready = sem("k0T_ready"), sem("v0T_ready"), sem("k1T_ready"), sem("v1T_ready")
        wq_h_ready, wo_h_ready, u_h_ready, v1_h_ready = sem("wq_h_ready"), sem("wo_h_ready"), sem("u_h_ready"), sem("v1_h_ready")
        a0_ready, c0_ready, bq0_ready, u_ready, v0o_ready = sem("a0_ready"), sem("c0_ready"), sem("bq0_ready"), sem("u_ready"), sem("v0o_ready")
        v0_h_ready, v0_ready, kd_h_ready, kd_ready = sem("v0_h_ready"), sem("v0_ready"), sem("kd_h_ready"), sem("kd_ready")
        v1_ready, wq_ready, wo_ready = sem("v1_ready"), sem("wq_ready"), sem("wo_ready")
        ident_zero, ident_ready, kd_zero, vd_zero, const_ready = sem("ident_zero"), sem("ident_ready"), sem("kd_zero"), sem("vd_zero"), sem("const_ready")
        q_done, s_done, t_done, pv_done, out_done = sem("q_done"), sem("s_done"), sem("t_done"), sem("pv_done"), sem("out_done")
        l0_done, p0t_done = sem("l0_done"), sem("p0t_done")
        qh_ready, exp_done, pth_ready, cth_ready = sem("qh_ready"), sem("exp_done"), sem("pth_ready"), sem("cth_ready")
        xh_ready, exp0_done, p0h_ready, z_done = sem("xh_ready"), sem("exp0_done"), sem("p0h_ready"), sem("z_done")
        ql_ready, max_done, sub_done, sum_done, rcp_done = sem("ql_ready"), sem("max_done"), sem("sub_done"), sem("sum_done"), sem("rcp_done")
        ptl_ready, ctl_ready, y_done, bn_done, nb_done = sem("ptl_ready"), sem("ctl_ready"), sem("y_done"), sem("bn_done"), sem("nb_done")
        both_done, diff_done, within_done, between_done, var_done = sem("both_done"), sem("diff_done"), sem("within_done"), sem("between_done"), sem("var_done")
        neg0_done, kept0_done = sem("neg0_done"), sem("kept0_done")
        add0_done, sel0_done, max0_done, sub0_done = sem("add0_done"), sem("sel0_done"), sem("max0_done"), sem("sub0_done")
        sum0_done, rcp0_done, prob0_done, p0l_ready = sem("sum0_done"), sem("rcp0_done"), sem("prob0_done"), sem("p0l_ready")
        prob_done, xl_ready = sem("prob_done"), sem("xl_ready")
        rs_done, gamma_done, beta_done = sem("rs_done"), sem("gamma_done"), sem("beta_done")

        def units(i, k):
            return TURN * i + k

        def tiles(i, k, t):
            return TILES * TURN * i + TILES * k + t

        def chunks(i, k, c):
            return KC * TURN * i + KC * k + c

        def blocks(i, b):
            return 2 * i + b

        def wait(eng, semaphore, count):
            if not (type(count) is int and count <= 0):
                eng.wait_ge(semaphore, count)

        def unit_exists(i, k):
            return type(i) is not int or 0 <= k < UNITS

        def block_exists(i, b):
            return type(i) is not int or 0 <= b < BLOCKS

        def run(eng, step):
            for k in range(FIRST):
                step(0, k)
            with eng.Fori(0, TURNS) as i:
                for k in range(FIRST, FIRST + TURN):
                    step(i, k)
            for k in range(LOOP_END, STEPS):
                step(0, k)

        def part3(a_h, a_l, b_h, b_l):
            return ((a_h, b_h), (a_l, b_h), (a_h, b_l))

        def f32(ap):
            return ap.bitcast(F32)

        def wide(ap, n):
            return ap.unsqueeze(2).to_broadcast([ap.shape[0], ap.shape[1], n])

        block = ctx.enter_context(nc.Block())

        @block.sync
        def _(sp):
            sp.dma_start(ctxT_sb[:], ctxT.rearrange("(c p) k -> p c k", p=P)).then_inc(ld_ctx, 16)
            sp.dma_start(raw0[:], w0k.rearrange("(c p) e -> p c e", p=P)).then_inc(ld_w0k, 16)
            sp.dma_start(raw1[:], w0q.rearrange("(c p) e -> p c e", p=P)).then_inc(ld_w0q, 16)
            sp.dma_start(x_raw[:].rearrange("p c t -> p (c t)"), xT[0, 0]).then_inc(ld_xT, 16)
            sp.dma_start(raw2[:], w0v.rearrange("(c p) e -> p c e", p=P)).then_inc(ld_w0v, 16)
            sp.dma_start(raw3[:], w1q.rearrange("(c p) e -> p c e", p=P)).then_inc(ld_w1q, 16)
            sp.wait_ge(mm_k0T, 2)
            sp.dma_start(raw0[:], w1k.rearrange("(c p) e -> p c e", p=P)).then_inc(ld_w1k, 16)
            sp.wait_ge(mm_a0, 2)
            sp.dma_start(raw1[:], w1v.rearrange("(c p) e -> p c e", p=P)).then_inc(ld_w1v, 16)
            sp.wait_ge(mm_v0T, 2)
            sp.dma_start(raw2[:], w1o.rearrange("(c p) e -> p c e", p=P)).then_inc(ld_w1o, 16)
            sp.wait_ge(vd_zero, 2)
            sp.wait_ge(v1_h_ready, BATCH)
            sp.wait_ge(v1_ready, BATCH)
            for part, blocks_of in ((v1_h, vd_h), (v1_l, vd_l)):
                for c in range(KC):
                    done = KSTART[c] if c == 0 else KSTART[c - 1] + KROWS
                    while done < KSTART[c] + KROWS:
                        head, key = divmod(done, KEYS)
                        m = min(KEYS - key, KSTART[c] + KROWS - done)
                        r = done - KSTART[c]
                        own = slice(head * HEAD_DIM, (head + 1) * HEAD_DIM)
                        sp.dma_start(
                            f32(blocks_of[r:r + m]).rearrange("r b g c d -> r (b g) c d")[:, :, c, own],
                            f32(part[key:key + m]).rearrange("r b (g d) -> r (b g) d", d=P)[:, :, own],
                        ).then_inc(vd_placed, 16)
                        done += m

            def next_inputs(i, b):
                if not block_exists(i, b + 1):
                    return
                j = i + (b + 1) // 2
                wait(sp, xl_ready, CH * blocks(i, b + 1))
                wait(sp, sel0_done, blocks(i, b + 1))
                sp.dma_start(x_raw[:].rearrange("p c t -> p (c t)"), xT[(b + 1) % 2, j]).then_inc(ld_xT, 16)
                sp.dma_start(mask_sb[:].rearrange("p t k -> p (t k)"), mask[(b + 1) % 2, j]).then_inc(ld_mask, 16)

            def store(i, b):
                for t in range(TILES):
                    wait(sp, beta_done, TILES * blocks(i, b) + t + 1)
                    sp.dma_start(out[b % 2, i + b // 2, t], y[:, t, :]).then_inc(stored[t], 16)

            def rows_of_x(i, b):
                if b > 0:
                    wait(sp, y_done, TILES * blocks(i, b))
                sp.dma_start(x_nat[:], x[b % 2, i + b // 2]).then_inc(ld_x, 16)

            next_inputs(0, 0)
            sp.wait_ge(mm_u, BATCH)
            sp.wait_ge(wq_ready, CH)
            rows_of_x(0, 0)
            with sp.Fori(0, TURNS) as i:
                for b in (1, 2):
                    next_inputs(i, b)
                    store(i, b - 1)
                    rows_of_x(i, b)
            store(0, BLOCKS - 2)
            rows_of_x(0, BLOCKS - 1)
            store(0, BLOCKS - 1)
            for t in range(TILES):
                sp.wait_ge(stored[t], 16 * BLOCKS)

        @block.gpsimd
        def _(pool):
            def x_rest(i, b, c):
                if not block_exists(i, b):
                    return
                wait(pool, xh_ready, CH * blocks(i, b) + c + 1)
                nc.gpsimd.tensor_tensor(x_l[:, c], x_raw[:, c], f32(x_h[:, c]), ALU.subtract).then_inc(xl_ready, 1)

            nc.gpsimd.memset(ident[:], 0.0).then_inc(ident_zero, 1)
            pool.wait_ge(ident_zero, 1)
            nc.gpsimd.affine_select(out=ident[:], in_=ident[:], compare_op=ALU.not_equal, fill=1.0, base=0,
                                    pattern=[[-1, P]], channel_multiplier=1).then_inc(ident_ready, 1)
            nc.gpsimd.memset(minus_half[:], -0.5).then_inc(const_ready, 1)
            for part in (kd_h, kd_l):
                nc.gpsimd.memset(f32(part[:]), 0.0).then_inc(kd_zero, 1)
            for c in range(CH):
                x_rest(0, 0, c)
            for part in (vd_h, vd_l):
                nc.gpsimd.memset(f32(part[:]), 0.0).then_inc(vd_zero, 1)
            for c in range(CH):
                pool.wait_ge(wo_h_ready, c + 1)
                nc.gpsimd.tensor_tensor(wo_l[:, c], raw2[:, c], f32(wo_h[:, c]), ALU.subtract).then_inc(wo_ready, 1)

            def scale_probs(i, k, t):
                if not unit_exists(i, k):
                    return
                wait(pool, rcp_done, tiles(i, k, t) + 1)
                ap = prob[:, k % 2, t].rearrange("p (h k) -> p h k", k=KEYS)
                nc.gpsimd.tensor_tensor(ap, ap, wide(rc[:, k % 2, t], KEYS), ALU.mult).then_inc(prob_done, 1)

            def root(i, b):
                if not block_exists(i, b):
                    return
                wait(pool, var_done, blocks(i, b) + 1)
                nc.gpsimd.tensor_tensor(rs[:], ve[:], minus_half[:], ALU.pow).then_inc(rs_done, 1)

            def affine(i, b, t):
                if not block_exists(i, b):
                    return
                m = TILES * blocks(i, b) + t
                wait(pool, z_done, m + 1)
                nc.gpsimd.tensor_tensor(y[:, t], y[:, t], rows_sb[:, 0], ALU.mult).then_inc(gamma_done, 1)
                wait(pool, gamma_done, m + 1)
                nc.gpsimd.tensor_tensor(y[:, t], y[:, t], rows_sb[:, 1], ALU.add).then_inc(beta_done, 1)

            def step(i, k):
                g, b = k % CH, k // CH
                scale_probs(i, k - 1, 3)
                if g == 3:
                    affine(i, b - 1, 1)
                scale_probs(i, k, 0)
                if g == 2:
                    root(i, b - 1)
                if g == 3:
                    affine(i, b - 1, 2)
                scale_probs(i, k, 1)
                if g == 2:
                    for c in range(CH):
                        x_rest(i, b + 1, c)
                if g == 3:
                    affine(i, b - 1, 3)
                scale_probs(i, k, 2)
                if g == 2:
                    affine(i, b - 1, 0)

            pool.wait_ge(ld_rows, 16)
            pool.wait_ge(const_ready, 1)
            run(pool, step)

        @block.scalar
        def _(act):
            act.dma_start(cols_sb[:].rearrange("p a c -> p (a c)"), cols).then_inc(ld_cols, 16)
            act.dma_start(mask_sb[:].rearrange("p t k -> p (t k)"), mask[0, 0]).then_inc(ld_mask, 16)
            act.dma_start(rows_sb[:].rearrange("p a d -> p (a d)"),
                          rows.rearrange("(o n) -> o n", o=1).to_broadcast([P, 3 * DIM])).then_inc(ld_rows, 16)

            def leave(banks, made, to, bias, ready):
                for c in range(CH):
                    act.wait_ge(made, c // 2 + 1)
                    src = banks[c // 2][:, 0:2 * BATCH * KEYS].rearrange("p (e k) -> p e k", e=2)[:, c % 2]
                    nc.scalar.activation(to[:, c], src, ACT.Identity, bias=cols_sb[:, bias, c:c + 1]).then_inc(ready, 1)

            def round_x(i, b):
                if not block_exists(i, b):
                    return
                wait(act, ld_xT, 16 * (blocks(i, b) + 1))
                wait(act, q_done, CH * blocks(i, b))
                for c in range(CH):
                    nc.scalar.activation(x_h[:, c], x_raw[:, c], ACT.Copy).then_inc(xh_ready, 1)

            def exp0(i, b):
                if not block_exists(i, b):
                    return
                wait(act, sub0_done, blocks(i, b) + 1)
                wait(act, p0t_done, blocks(i, b))
                nc.scalar.activation(e0[:], m0[:], ACT.Exp).then_inc(exp0_done, 1)

            def round_p0(i, b):
                if not block_exists(i, b):
                    return
                wait(act, p0t_done, blocks(i, b) + 1)
                nc.scalar.activation(p0_h[:, b % 2], ps_0[0:KEYS, :], ACT.Copy).then_inc(p0h_ready, 1)

            def round_q(i, k):
                if not unit_exists(i, k):
                    return
                wait(act, q_done, units(i, k) + 1)
                nc.scalar.activation(q_h[:, k % 2], ps_q[:], ACT.Identity,
                                     bias=cols_sb[:, 3, k % CH:k % CH + 1]).then_inc(qh_ready, 1)

            act.wait_ge(ld_cols, 16)
            leave(bank[1:3], mm_k0T, k0T, 1, k0T_ready)
            round_x(0, 0)
            leave(bank[5:7], mm_v0T, v0T, 2, v0T_ready)
            exp0(0, 0)
            act.wait_ge(ld_w1q, 16)
            for c in range(CH):
                nc.scalar.activation(wq_h[:, c], raw3[:, c], ACT.Copy).then_inc(wq_h_ready, 1)
            for b in range(BATCH):
                act.wait_ge(mm_u, b + 1)
                nc.scalar.activation(u_h[:, b], bank[1 + b][0:KEYS, :], ACT.Copy).then_inc(u_h_ready, 1)
            leave(bank[5:7], mm_k1T, k1T, 4, k1T_ready)
            leave(bank[3:5], mm_v1T, v1T, 5, v1T_ready)
            round_p0(0, 0)
            for b in range(BATCH):
                act.wait_ge(mm_v1, b + 1)
                nc.scalar.activation(v1_h[:, b], bank[5 + b][0:KEYS, :], ACT.Copy).then_inc(v1_h_ready, 1)
            round_q(0, 0)
            act.wait_ge(ld_w1o, 16)
            for c in range(CH):
                nc.scalar.activation(wo_h[:, c], raw2[:, c], ACT.Copy).then_inc(wo_h_ready, 1)

            def exps(i, k, t):
                if not unit_exists(i, k):
                    return
                wait(act, sub_done, tiles(i, k, t) + 1)
                nc.scalar.activation(prob[:, k % 2, t], prob[:, k % 2, t], ACT.Exp, scale=SCALE).then_inc(exp_done, 1)

            def round_pt(i, k, c):
                if not unit_exists(i, k):
                    return
                if type(i) is int and k == 0 and c == 0:
                    act.wait_ge(vd_placed, 16 * 12)
                wait(act, t_done, chunks(i, k, c) + 1)
                nc.scalar.activation(pt_h[:, c], ps_t[c % 2][0:KROWS, :], ACT.Copy).then_inc(pth_ready, 1)

            def round_ct(i, k):
                if not unit_exists(i, k):
                    return
                wait(act, pv_done, units(i, k) + 1)
                nc.scalar.activation(ct_h[:, k % CH], ps_pv[:], ACT.Copy).then_inc(cth_ready, 1)

            def normalise(i, b, t):
                if not block_exists(i, b):
                    return
                wait(act, nb_done, blocks(i, b) + 1)
                nc.scalar.activation(y[:, t], y[:, t], ACT.Identity, bias=nb[:, t:t + 1],
                                     scale=rs[:, t:t + 1]).then_inc(z_done, 1)

            def step(i, k):
                g, b = k % CH, k // CH
                exps(i, k, 0)
                round_ct(i, k - 2)
                if g == 3:
                    normalise(i, b - 1, 1)
                exps(i, k, 1)
                round_pt(i, k - 1, 0)
                if g == 3:
                    normalise(i, b - 1, 2)
                if g == 2:
                    exp0(i, b + 1)
                round_q(i, k + 1)
                exps(i, k, 2)
                round_pt(i, k - 1, 1)
                if g == 3:
                    normalise(i, b - 1, 3)
                if g == 2:
                    round_x(i, b + 1)
                exps(i, k, 3)
                round_pt(i, k - 1, 2)
                if g == 2:
                    round_p0(i, b + 1)
                    normalise(i, b - 1, 0)

            run(act, step)

        @block.vector
        def _(dve):
            def layer0_scores(i, b):
                if not block_exists(i, b):
                    return
                n = blocks(i, b)
                v = slice(b % 2 * KEYS, (b % 2 + 1) * KEYS)
                wait(dve, l0_done, n + 1)
                nc.vector.tensor_tensor(s0[:], ps_0[:, 0:TILES * KEYS].rearrange("p (t k) -> p t k", k=KEYS),
                                        c0[:, v].unsqueeze(1).to_broadcast([P, TILES, KEYS]), ALU.add).then_inc(add0_done, 1)
                wait(dve, ld_mask, 16 * (n + 1))
                nc.vector.tensor_scalar(n0[:], mask_sb[:], 0.0, NEG, ALU.is_equal, ALU.mult).then_inc(neg0_done, 1)
                wait(dve, add0_done, n + 1)
                wait(dve, neg0_done, n + 1)
                nc.vector.scalar_tensor_tensor(out=s0[:], in0=n0[:], scalar=0.0, in1=s0[:],
                                               op0=ALU.is_equal, op1=ALU.mult).then_inc(kept0_done, 1)
                wait(dve, kept0_done, n + 1)
                wait(dve, exp0_done, n)
                nc.vector.tensor_tensor(m0[:], s0[:], n0[:], ALU.add).then_inc(sel0_done, 1)
                wait(dve, sel0_done, n + 1)
                nc.vector.reduce_max(stat0[:, 0], m0[:], AX_X).then_inc(max0_done, 1)
                wait(dve, max0_done, n + 1)
                nc.vector.tensor_tensor(m0[:], m0[:], wide(stat0[:, 0], KEYS), ALU.subtract).then_inc(sub0_done, 1)

            def layer0_probs(i, b):
                if not block_exists(i, b):
                    return
                n = blocks(i, b)
                wait(dve, exp0_done, n + 1)
                nc.vector.reduce_sum(stat0[:, 1], e0[:], AX_X).then_inc(sum0_done, 1)
                wait(dve, sum0_done, n + 1)
                nc.vector.reciprocal(stat0[:, 2], stat0[:, 1]).then_inc(rcp0_done, 1)
                wait(dve, rcp0_done, n + 1)
                nc.vector.tensor_tensor(e0[:], e0[:], wide(stat0[:, 2], KEYS), ALU.mult).then_inc(prob0_done, 1)

            def p0_rest(i, b):
                if not block_exists(i, b):
                    return
                wait(dve, p0h_ready, blocks(i, b) + 1)
                nc.vector.tensor_tensor(p0_l[:, b % 2], ps_0[0:KEYS, :], f32(p0_h[:, b % 2]),
                                        ALU.subtract).then_inc(p0l_ready, 1)

            def q_rest(i, k):
                if not unit_exists(i, k):
                    return
                wait(dve, qh_ready, units(i, k) + 1)
                nc.vector.scalar_tensor_tensor(out=q_l[:, k % 2], in0=ps_q[:], scalar=cols_sb[:, 3, k % CH:k % CH + 1],
                                               in1=f32(q_h[:, k % 2]), op0=ALU.add, op1=ALU.subtract).then_inc(ql_ready, 1)

            dve.wait_ge(ld_cols, 16)
            nc.vector.tensor_copy(bq0_wide[:], wide(cols_sb[:, 0], P)).then_inc(bq0_ready, 1)
            for h in range(2):
                dve.wait_ge(mm_a0, h + 1)
                nc.vector.tensor_copy(a0[:, 2 * h:2 * h + 2].rearrange("p c k -> p (c k)"),
                                      bank[3 + h][:, 0:2 * BATCH * KEYS]).then_inc(a0_ready, 1)
            dve.wait_ge(mm_c0, 1)
            nc.vector.tensor_copy(c0[:], ps_0[:, 0:BATCH * KEYS]).then_inc(c0_ready, 1)
            dve.wait_ge(c0_ready, 1)
            layer0_scores(0, 0)
            for c in range(CH):
                dve.wait_ge(wq_h_ready, c + 1)
                nc.vector.tensor_tensor(wq_l[:, c], raw3[:, c], f32(wq_h[:, c]), ALU.subtract).then_inc(wq_ready, 1)
            layer0_probs(0, 0)
            dve.wait_ge(ld_rows, 16)
            for b in range(BATCH):
                dve.wait_ge(mm_v0, b + 1)
                nc.vector.tensor_tensor(v0o[:, b], bank[3 + b][0:KEYS, :], rows_sb[0:KEYS, 2], ALU.add).then_inc(v0o_ready, 1)
            for b in range(BATCH):
                dve.wait_ge(u_h_ready, b + 1)
                nc.vector.tensor_tensor(u_l[:, b], bank[1 + b][0:KEYS, :], f32(u_h[:, b]), ALU.subtract).then_inc(u_ready, 1)
            for b in range(BATCH):
                dve.wait_ge(v0o_ready, b + 1)
                nc.vector.tensor_copy(v0_h[:, b], v0o[:, b]).then_inc(v0_h_ready, 1)
            for b in range(BATCH):
                dve.wait_ge(v0_h_ready, b + 1)
                nc.vector.tensor_tensor(v0_l[:, b], v0o[:, b], f32(v0_h[:, b]), ALU.subtract).then_inc(v0_ready, 1)
            dve.wait_ge(kd_zero, 2)
            dve.wait_ge(k1T_ready, CH)
            for h in range(GROUP_HEADS):
                own, at = slice(h * HEAD_DIM, (h + 1) * HEAD_DIM), slice(h * KEYS, (h + 1) * KEYS)
                nc.vector.tensor_copy(kd_h[own, :, :, at],
                                      k1T[own].rearrange("p c (b k) -> p b c k", b=BATCH)).then_inc(kd_h_ready, 1)
            for h in range(GROUP_HEADS):
                own, at = slice(h * HEAD_DIM, (h + 1) * HEAD_DIM), slice(h * KEYS, (h + 1) * KEYS)
                dve.wait_ge(kd_h_ready, h + 1)
                nc.vector.tensor_tensor(kd_l[own, :, :, at], k1T[own].rearrange("p c (b k) -> p b c k", b=BATCH),
                                        f32(kd_h[own, :, :, at]), ALU.subtract).then_inc(kd_ready, 1)
            p0_rest(0, 0)
            for b in range(BATCH):
                dve.wait_ge(v1_h_ready, b + 1)
                nc.vector.tensor_tensor(v1_l[:, b], bank[5 + b][0:KEYS, :], f32(v1_h[:, b]), ALU.subtract).then_inc(v1_ready, 1)
            q_rest(0, 0)

            def scores_minus_max(i, k, t):
                if not unit_exists(i, k):
                    return
                wait(dve, s_done, tiles(i, k, t) + 1)
                scores = ps_s[t % 2][:, 0:GCOLS].rearrange("p (h k) -> p h k", k=KEYS)
                nc.vector.reduce_max(mx[:, k % 2, t], scores, AX_X).then_inc(max_done, 1)
                wait(dve, max_done, tiles(i, k, t) + 1)
                nc.vector.tensor_tensor(prob[:, k % 2, t].rearrange("p (h k) -> p h k", k=KEYS), scores,
                                        wide(mx[:, k % 2, t], KEYS), ALU.subtract).then_inc(sub_done, 1)

            def sums(i, k, t):
                if not unit_exists(i, k):
                    return
                wait(dve, exp_done, tiles(i, k, t) + 1)
                nc.vector.reduce_sum(sm[:, k % 2, t], prob[:, k % 2, t].rearrange("p (h k) -> p h k", k=KEYS),
                                     AX_X).then_inc(sum_done, 1)
                wait(dve, sum_done, tiles(i, k, t) + 1)
                nc.vector.reciprocal(rc[:, k % 2, t], sm[:, k % 2, t]).then_inc(rcp_done, 1)

            def pt_rest(i, k, c):
                if not unit_exists(i, k):
                    return
                wait(dve, pth_ready, chunks(i, k, c) + 1)
                nc.vector.tensor_tensor(pt_l[:, c], ps_t[c % 2][0:KROWS, :], f32(pt_h[:, c]),
                                        ALU.subtract).then_inc(ptl_ready, 1)

            def ct_rest(i, k):
                if not unit_exists(i, k):
                    return
                wait(dve, cth_ready, units(i, k) + 1)
                nc.vector.tensor_tensor(ct_l[:, k % CH], ps_pv[:], f32(ct_h[:, k % CH]), ALU.subtract).then_inc(ctl_ready, 1)

            def residual(i, b, t):
                if not block_exists(i, b):
                    return
                m = TILES * blocks(i, b) + t
                wait(dve, out_done, m + 1)
                if t == 0:
                    wait(dve, ld_x, 16 * (blocks(i, b) + 1))
                wait(dve, stored[t], 16 * blocks(i, b))
                nc.vector.tensor_tensor(y[:, t], ps_out[:], x_nat[:, t], ALU.add).then_inc(y_done, 1)
                wait(dve, y_done, m + 1)
                nc.vector.bn_stats(bn6[:, t], y[:, t]).then_inc(bn_done, 1)

            def variance(i, b):
                if not block_exists(i, b):
                    return
                n = blocks(i, b)
                wait(dve, bn_done, TILES * (n + 1))
                nc.vector.tensor_tensor(both[:], bn6[:, :, 0:3], bn6[:, :, 3:6], ALU.add).then_inc(both_done, 1)
                nc.vector.tensor_tensor(diff[:], bn6[:, :, 1], bn6[:, :, 4], ALU.subtract).then_inc(diff_done, 1)
                wait(dve, both_done, n + 1)
                nc.vector.tensor_scalar(within[:], both[:, :, 2], 1.0 / DIM, LN_EPS, ALU.mult, ALU.add).then_inc(within_done, 1)
                wait(dve, diff_done, n + 1)
                nc.vector.scalar_tensor_tensor(out=between[:], in0=diff[:], scalar=0.25, in1=diff[:],
                                               op0=ALU.mult, op1=ALU.mult).then_inc(between_done, 1)
                wait(dve, within_done, n + 1)
                wait(dve, between_done, n + 1)
                nc.vector.tensor_tensor(ve[:], within[:], between[:], ALU.add).then_inc(var_done, 1)

            def offset(i, b):
                if not block_exists(i, b):
                    return
                wait(dve, rs_done, blocks(i, b) + 1)
                nc.vector.scalar_tensor_tensor(out=nb[:], in0=both[:, :, 1], scalar=-0.5, in1=rs[:],
                                               op0=ALU.mult, op1=ALU.mult).then_inc(nb_done, 1)

            def step(i, k):
                g, b = k % CH, k // CH
                scores_minus_max(i, k, 0)
                sums(i, k - 1, 3)
                if g == 2:
                    residual(i, b - 1, 2)
                ct_rest(i, k - 2)
                scores_minus_max(i, k, 1)
                sums(i, k, 0)
                pt_rest(i, k - 1, 0)
                if g == 2:
                    residual(i, b - 1, 3)
                    variance(i, b - 1)
                    layer0_scores(i, b + 1)
                scores_minus_max(i, k, 2)
                q_rest(i, k + 1)
                sums(i, k, 1)
                pt_rest(i, k - 1, 1)
                if g == 1:
                    residual(i, b - 1, 0)
                if g == 2:
                    offset(i, b - 1)
                    layer0_probs(i, b + 1)
                scores_minus_max(i, k, 3)
                sums(i, k, 2)
                pt_rest(i, k - 1, 2)
                if g == 1:
                    residual(i, b - 1, 1)
                if g == 2:
                    p0_rest(i, b + 1)

            run(dve, step)

        @block.tensor
        def _(pe):
            def project(banks, weights, moving, made):
                for e in range(CH):
                    for c in range(CH):
                        mm = nc.tensor.matmul(banks[e // 2][:, (e % 2) * BATCH * KEYS:(e % 2 + 1) * BATCH * KEYS],
                                              weights[:, c, e * P:(e + 1) * P], moving[:, c],
                                              start=(c == 0), stop=(c == CH - 1))
                    if e % 2:
                        mm.then_inc(made, 1)

            def to_rows(banks, src, made):
                for b in range(BATCH):
                    for e in range(CH):
                        mm = nc.tensor.transpose(banks[b][0:KEYS, e * P:(e + 1) * P],
                                                 src[:, e, b * KEYS:(b + 1) * KEYS], ident[:])
                    mm.then_inc(made, 1)

            def layer0(i, b):
                if not block_exists(i, b):
                    return
                wait(pe, ld_xT, 16 * (blocks(i, b) + 1))
                wait(pe, p0l_ready, blocks(i, b))
                for t in range(TILES):
                    for c in range(CH):
                        mm = nc.tensor.matmul(ps_0[:, t * KEYS:(t + 1) * KEYS], x_raw[:, c, t * P:(t + 1) * P],
                                              a0[:, c, b % 2 * KEYS:(b % 2 + 1) * KEYS],
                                              start=(c == 0), stop=(c == CH - 1))
                mm.then_inc(l0_done, 1)

            def transpose0(i, b):
                if not block_exists(i, b):
                    return
                wait(pe, prob0_done, blocks(i, b) + 1)
                for t in range(TILES):
                    mm = nc.tensor.transpose(ps_0[0:KEYS, t * P:(t + 1) * P], e0[:, t], ident[:])
                mm.then_inc(p0t_done, 1)

            def query(i, k, first, last):
                if not unit_exists(i, k):
                    return
                b, g = k // CH, k % CH
                own = slice(g * P, (g + 1) * P)
                if first == 0:
                    wait(pe, ql_ready, units(i, k))
                for m in range(first, last):
                    c, part = divmod(m, 3)
                    if c < CH:
                        if g == 0 and part == 0:
                            wait(pe, xl_ready, CH * blocks(i, b) + c + 1)
                        w, v = part3(wq_h[:, c, own], wq_l[:, c, own], x_h[:, c], x_l[:, c])[part]
                    else:
                        if g == 0 and part == 0:
                            wait(pe, p0l_ready, blocks(i, b) + 1)
                        w, v = part3(u_h[:, b % 2, own], u_l[:, b % 2, own], p0_h[:, b % 2], p0_l[:, b % 2])[part]
                    mm = nc.tensor.matmul(ps_q[:], w, v, start=(m == 0), stop=(m == 3 * CH + 2))
                if last == 3 * CH + 3:
                    mm.then_inc(q_done, 1)

            def scores(i, k, t):
                if not unit_exists(i, k):
                    return
                b, g = k // CH, k % CH
                if t == 0:
                    wait(pe, ql_ready, units(i, k) + 1)
                wait(pe, sub_done, tiles(i, k, t) - 1)
                own = slice(t * P, (t + 1) * P)
                for m, (w, v) in enumerate(part3(q_h[:, k % 2, own], q_l[:, k % 2, own], kd_h[:, b % 2, g], kd_l[:, b % 2, g])):
                    mm = nc.tensor.matmul(ps_s[t % 2][:, 0:GCOLS], w, v, start=(m == 0), stop=(m == 2))
                mm.then_inc(s_done, 1)

            def transposes(i, k, c):
                if not unit_exists(i, k):
                    return
                if c == 0:
                    wait(pe, prob_done, tiles(i, k, TILES))
                wait(pe, ptl_ready, chunks(i, k, c) - (0, 2, 1)[c])
                for t in range(TILES):
                    mm = nc.tensor.transpose(ps_t[c % 2][0:KROWS, t * P:(t + 1) * P],
                                             prob[:, k % 2, t, KSTART[c]:KSTART[c] + KROWS], ident[:])
                mm.then_inc(t_done, 1)

            def context(i, k, c):
                if not unit_exists(i, k):
                    return
                b, g = k // CH, k % CH
                if c == 0:
                    wait(pe, ctl_ready, units(i, k))
                wait(pe, ptl_ready, chunks(i, k, c) + 1)
                for m, (w, v) in enumerate(part3(vd_h[:, b % 2, g, c], vd_l[:, b % 2, g, c], pt_h[:, c], pt_l[:, c])):
                    mm = nc.tensor.matmul(ps_pv[:], w, v, start=(c == 0 and m == 0), stop=(c == KC - 1 and m == 2))
                if c == KC - 1:
                    mm.then_inc(pv_done, 1)

            def output(i, b, t):
                if not block_exists(i, b):
                    return
                own = slice(t * P, (t + 1) * P)
                wait(pe, y_done, TILES * blocks(i, b) + t)
                for m, (w, v) in enumerate(part3(p0_h[:, b % 2, own], p0_l[:, b % 2, own], v0_h[:, b % 2], v0_l[:, b % 2])):
                    nc.tensor.matmul(ps_out[:], w, v, start=(m == 0), stop=False)
                if t == 0:
                    wait(pe, ctl_ready, CH * (blocks(i, b) + 1))
                for c in range(CH):
                    for m, (w, v) in enumerate(part3(ct_h[:, c, own], ct_l[:, c, own], wo_h[:, c], wo_l[:, c])):
                        mm = nc.tensor.matmul(ps_out[:], w, v, start=False, stop=(c == CH - 1 and m == 2))
                mm.then_inc(out_done, 1)

            pe.wait_ge(ld_ctx, 16)
            pe.wait_ge(ld_w0k, 16)
            project(bank[1:3], raw0, ctxT_sb, mm_k0T)
            pe.wait_ge(ld_w0q, 16)
            pe.wait_ge(k0T_ready, CH)
            project(bank[3:5], raw1, k0T, mm_a0)
            pe.wait_ge(bq0_ready, 1)
            for c in range(CH):
                mm = nc.tensor.matmul(ps_0[:, 0:BATCH * KEYS], bq0_wide[:, c], k0T[:, c], start=(c == 0), stop=(c == CH - 1))
            mm.then_inc(mm_c0, 1)
            pe.wait_ge(ld_w0v, 16)
            project(bank[5:7], raw2, ctxT_sb, mm_v0T)
            pe.wait_ge(a0_ready, 2)
            pe.wait_ge(c0_ready, 1)
            layer0(0, 0)
            pe.wait_ge(v0T_ready, CH)
            pe.wait_ge(ident_ready, 1)
            to_rows(bank[3:5], v0T, mm_v0)
            pe.wait_ge(ld_w1q, 16)
            for b in range(BATCH):
                for c in range(CH):
                    mm = nc.tensor.matmul(bank[1 + b][0:KEYS, :], v0T[:, c, b * KEYS:(b + 1) * KEYS], raw3[:, c],
                                          start=(c == 0), stop=(c == CH - 1))
                mm.then_inc(mm_u, 1)
            pe.wait_ge(ld_w1k, 16)
            project(bank[5:7], raw0, ctxT_sb, mm_k1T)
            transpose0(0, 0)
            pe.wait_ge(v0o_ready, BATCH)
            pe.wait_ge(ld_w1v, 16)
            project(bank[3:5], raw1, ctxT_sb, mm_v1T)
            pe.wait_ge(wq_ready, CH)
            pe.wait_ge(u_ready, BATCH)
            query(0, 0, 0, 3 * CH + 3)
            pe.wait_ge(k1T_ready, CH)
            pe.wait_ge(v1T_ready, CH)
            to_rows(bank[5:7], v1T, mm_v1)
            pe.wait_ge(kd_ready, GROUP_HEADS)

            def step(i, k):
                g, b = k % CH, k // CH
                scores(i, k, 0)
                query(i, k + 1, 0, 8)
                if g == 2:
                    output(i, b - 1, 3)
                if type(i) is int and k == 2:
                    pe.wait_ge(vd_placed, 16 * 12)
                context(i, k - 2, 2)
                if g == 2:
                    layer0(i, b + 1)
                scores(i, k, 1)
                transposes(i, k - 1, 0)
                query(i, k + 1, 8, 15)
                if g == 1:
                    output(i, b - 1, 0)
                scores(i, k, 2)
                transposes(i, k - 1, 1)
                if type(i) is int and k == 1:
                    pe.wait_ge(v0_ready, BATCH)
                context(i, k - 1, 0)
                if g == 1:
                    output(i, b - 1, 1)
                scores(i, k, 3)
                transposes(i, k - 1, 2)
                context(i, k - 1, 1)
                if g == 1:
                    output(i, b - 1, 2)
                if g == 2:
                    transpose0(i, b + 1)

            run(pe, step)


def kernel(**inputs):
    import numpy as np
    import concourse.bacc as bacc
    from concourse.bass_utils import run_bass_kernel_spmd

    def arr(name):
        return np.asarray(inputs[name])

    x, ctx, mask = arr("x"), arr("ctx_1024"), arr("mask_BxSxS2_ik0")
    w_qkv, b_qkv = arr("L1_xattn_W_qkv"), arr("L1_xattn_b_qkv")
    nj = SEQ // BLOCK
    by_channel = [arr("L0_xattn_bq"), arr("L0_xattn_bk"), arr("L0_xattn_bv"), b_qkv[:DIM], b_qkv[DIM:2 * DIM], b_qkv[2 * DIM:]]
    arrays = {
        "xT": x.reshape(BATCH, nj, BLOCK, CH, P).transpose(0, 1, 4, 3, 2).reshape(BATCH, nj, P, CH * BLOCK),
        "x": x,
        "mask": mask.reshape(BATCH, nj, TILES, P, KEYS).transpose(0, 1, 3, 2, 4).reshape(BATCH, nj, P, TILES * KEYS),
        "ctxT": ctx.reshape(BATCH * KEYS, DIM).T,
        "w0k": arr("L0_xattn_Wk").T, "w0q": arr("L0_xattn_Wq"), "w0v": arr("L0_xattn_Wv").T,
        "w1q": w_qkv[:DIM].T, "w1k": w_qkv[DIM:2 * DIM].T, "w1v": w_qkv[2 * DIM:].T, "w1o": arr("L1_xattn_W_o").T,
        "cols": np.stack(by_channel).reshape(6, CH, P).transpose(2, 0, 1).reshape(P, 6 * CH),
        "rows": np.concatenate([arr("L1_xattn_ln_gamma"), arr("L1_xattn_ln_beta"), arr("L1_xattn_b_o")]),
    }
    arrays = {"in_" + n: np.ascontiguousarray(a) for n, a in arrays.items()}
    nc = bacc.Bacc("TRN2", target_bir_lowering=False, num_devices=1)
    aps = {n[3:]: nc.dram_tensor(n, a.shape, mybir.dt.from_np(a.dtype), kind="ExternalInput").ap() for n, a in arrays.items()}
    out = nc.dram_tensor("out_0", (BATCH, SEQ, DIM), F32, kind="ExternalOutput").ap()
    aps["x"] = aps["x"].rearrange("b (j t p) d -> b j p t d", t=TILES, p=P)
    xattn_kernel(nc, **aps, out=out.rearrange("b (j t p) d -> b j t p d", t=TILES, p=P))
    r = run_bass_kernel_spmd(nc, [arrays], core_ids=[0])
    return r.results[0]["out_0"]
```

```python
from contextlib import ExitStack

import concourse.bass as bass
from concourse import mybir

F32 = mybir.dt.float32
F32R = mybir.dt.float32r
I32 = mybir.dt.int32
ALU = mybir.AluOpType
ACT = mybir.ActivationFunctionType
AX_X = mybir.AxisListType.X

BATCH, SEQ, DIM, KEYS = 2, 2048, 512, 77
HEADS = 16
HEAD_DIM = DIM // HEADS
P = 128
CH = DIM // P
GROUP_HEADS = P // HEAD_DIM
TILES = 4
BLOCK = TILES * P
BLOCKS = BATCH * SEQ // BLOCK
UNITS = BLOCKS * CH
GCOLS = GROUP_HEADS * KEYS
KC = 3
KROWS = -(-GCOLS // KC)
KSTART = [min(c * KROWS, GCOLS - KROWS) for c in range(KC)]
NEG = -1000000000.0
LN_EPS = 1e-05
SCALE = 1.0 / float(HEAD_DIM) ** 0.5
TURN = 2 * CH
FIRST = TURN
TURNS = 2
LOOP_END = FIRST + TURN * TURNS
SP_TURNS = 2
OUT_SHARE = [5, 5, 5, 8, 7, 8, 7, 4, 4, 4, 3, 0]
STEPS = UNITS + 6


def xattn_kernel(nc, xT, x, mask, ctxT, w0k, w0q, w0v, w1q, w1k, w1v, w1o, cols, rows, out):
    with ExitStack() as ctx:
        def sb(name, shape, dt=F32, stack=ctx):
            return stack.enter_context(nc.sbuf_tensor(name, shape, dt))

        def sem(name):
            return ctx.enter_context(nc.semaphore(name))

        with ExitStack() as prep:
            raw0 = sb("raw0", [P, CH, DIM], F32, prep)
            raw1 = sb("raw1", [P, CH, DIM], F32, prep)
            raw2 = sb("raw2", [P, CH, DIM], F32, prep)
            raw3 = sb("raw3", [P, CH, DIM], F32, prep)
            v1_h = sb("v1_h", [KEYS, BATCH, DIM], F32R, prep)
            v1_l = sb("v1_l", [KEYS, BATCH, DIM], F32R, prep)
            k0T = sb("k0T", [P, CH, BATCH * KEYS], F32, prep)
            v0T = sb("v0T", [P, CH, BATCH * KEYS], F32, prep)
            k1T = sb("k1T", [P, CH, BATCH * KEYS], F32, prep)
            v1T = sb("v1T", [P, CH, BATCH * KEYS], F32, prep)
            v0o = sb("v0o", [KEYS, BATCH, DIM], F32, prep)
            ctxT_sb = sb("ctxT_sb", [P, CH, BATCH * KEYS], F32, prep)
            bq0_wide = sb("bq0_wide", [P, CH, P], F32, prep)
            bo_sb = sb("bo_sb", [P, DIM], F32, prep)
        ct_h = sb("ct_h", [P, 2, CH, BLOCK], F32R)
        ct_l = sb("ct_l", [P, 2, CH, BLOCK], F32R)
        pt_h = sb("pt_h", [KROWS, KC, BLOCK], F32R)
        pt_l = sb("pt_l", [KROWS, KC, BLOCK], F32R)
        prob = sb("prob", [P, 2, TILES, GCOLS])
        y = sb("y", [P, TILES, DIM])

        wq_h = sb("wq_h", [P, CH, DIM], F32R)
        wq_l = sb("wq_l", [P, CH, DIM], F32R)
        wo_h = sb("wo_h", [P, CH, DIM], F32R)
        wo_l = sb("wo_l", [P, CH, DIM], F32R)
        a0 = sb("a0", [P, CH, BATCH * KEYS])
        c0 = sb("c0", [P, BATCH * KEYS])
        u_h = sb("u_h", [KEYS, BATCH, DIM], F32R)
        u_l = sb("u_l", [KEYS, BATCH, DIM], F32R)
        v0_h = sb("v0_h", [KEYS, BATCH, DIM], F32R)
        v0_l = sb("v0_l", [KEYS, BATCH, DIM], F32R)
        kd_h = sb("kd_h", [P, BATCH, CH, GCOLS], F32R)
        kd_l = sb("kd_l", [P, BATCH, CH, GCOLS], F32R)
        vd_h = sb("vd_h", [KROWS, BATCH, CH, KC, P], F32R)
        vd_l = sb("vd_l", [KROWS, BATCH, CH, KC, P], F32R)
        cols_sb = sb("cols_sb", [P, 6, CH])
        rows_sb = sb("rows_sb", [P, 2, DIM])
        bk1_scaled = sb("bk1_scaled", [P, CH])
        ident = sb("ident", [P, P])
        minus_half = sb("minus_half", [P, TILES])

        x_raw = sb("x_raw", [P, CH, BLOCK])
        x_h = sb("x_h", [P, CH, BLOCK], F32R)
        x_l = sb("x_l", [P, CH, BLOCK], F32R)
        mask_sb = sb("mask_sb", [P, TILES, KEYS], I32)
        n0 = sb("n0", [P, TILES, KEYS])
        m0 = sb("m0", [P, TILES, KEYS])
        e0 = sb("e0", [P, TILES, KEYS])
        stat0 = sb("stat0", [P, 3, TILES])
        p0_h = sb("p0_h", [KEYS, 2, BLOCK], F32R)
        p0_l = sb("p0_l", [KEYS, 2, BLOCK], F32R)
        q_h = sb("q_h", [P, 2, BLOCK], F32R)
        q_l = sb("q_l", [P, 2, BLOCK], F32R)
        mx = sb("mx", [P, 2, TILES, GROUP_HEADS])
        sm = sb("sm", [P, 2, TILES, GROUP_HEADS])
        rc = sb("rc", [P, 2, TILES, GROUP_HEADS])
        bn6 = sb("bn6", [P, TILES, 6])
        both = sb("both", [P, TILES, 3])
        diff = sb("diff", [P, TILES])
        within = sb("within", [P, TILES])
        between = sb("between", [P, TILES])
        ve = sb("ve", [P, TILES])
        rs = sb("rs", [P, TILES])
        nb = sb("nb", [P, TILES])

        bank = [ctx.enter_context(nc.psum_tensor(f"bank{n}", [P, 512], F32)) for n in range(8)]
        ps_q, ps_s, ps_t, ps_pv, ps_out, ps_0 = bank[0], bank[1:3], bank[3:5], bank[5], bank[6], bank[7]

        ld_ctx, ld_cols, ld_rows = sem("ld_ctx"), sem("ld_cols"), sem("ld_rows")
        ld_w0k, ld_w0q, ld_w0v, ld_w1q = sem("ld_w0k"), sem("ld_w0q"), sem("ld_w0v"), sem("ld_w1q")
        ld_w1k, ld_w1v, ld_w1o = sem("ld_w1k"), sem("ld_w1v"), sem("ld_w1o")
        ld_xT, ld_mask, ld_bo = sem("ld_xT"), sem("ld_mask"), sem("ld_bo")
        ld_x = [sem(f"ld_x{t}") for t in range(TILES)]
        vd_placed = sem("vd_placed")
        stored = [sem(f"stored{t}") for t in range(TILES)]
        mm_k0T, mm_a0, mm_c0, mm_v0T = sem("mm_k0T"), sem("mm_a0"), sem("mm_c0"), sem("mm_v0T")
        mm_v0, mm_u, mm_k1T, mm_v1T, mm_v1 = sem("mm_v0"), sem("mm_u"), sem("mm_k1T"), sem("mm_v1T"), sem("mm_v1")
        k0T_ready, v0T_ready, k1T_ready, v1T_ready = sem("k0T_ready"), sem("v0T_ready"), sem("k1T_ready"), sem("v1T_ready")
        wq_h_ready, wo_h_ready, u_h_ready, v1_h_ready = sem("wq_h_ready"), sem("wo_h_ready"), sem("u_h_ready"), sem("v1_h_ready")
        bk1_ready = sem("bk1_ready")
        a0_ready, c0_ready, bq0_ready, u_ready, v0o_ready = sem("a0_ready"), sem("c0_ready"), sem("bq0_ready"), sem("u_ready"), sem("v0o_ready")
        v0_h_ready, v0_ready, kd_h_ready, kd_ready = sem("v0_h_ready"), sem("v0_ready"), sem("kd_h_ready"), sem("kd_ready")
        v1_ready, wq_ready, wo_ready = sem("v1_ready"), sem("wq_ready"), sem("wo_ready")
        ident_zero, ident_ready, kd_zero, vd_zero, const_ready = sem("ident_zero"), sem("ident_ready"), sem("kd_zero"), sem("vd_zero"), sem("const_ready")
        q_done, s_done, t_done, pv_done, out_done = sem("q_done"), sem("s_done"), sem("t_done"), sem("pv_done"), sem("out_done")
        l0_done, p0t_done = sem("l0_done"), sem("p0t_done")
        qh_ready, exp_done, pth_ready, cth_ready = sem("qh_ready"), sem("exp_done"), sem("pth_ready"), sem("cth_ready")
        xh_ready, exp0_done, p0h_ready, z_done = sem("xh_ready"), sem("exp0_done"), sem("p0h_ready"), sem("z_done")
        ql_ready, max_done, sum_done, rcp_done = sem("ql_ready"), sem("max_done"), sem("sum_done"), sem("rcp_done")
        ptl_ready, ctl_ready, y_done, bn_done, nb_done = sem("ptl_ready"), sem("ctl_ready"), sem("y_done"), sem("bn_done"), sem("nb_done")
        both_done, diff_done, within_done, between_done, var_done = sem("both_done"), sem("diff_done"), sem("within_done"), sem("between_done"), sem("var_done")
        neg0_done, kept0_done = sem("neg0_done"), sem("kept0_done")
        add0_done, sel0_done, max0_done, sub0_done = sem("add0_done"), sem("sel0_done"), sem("max0_done"), sem("sub0_done")
        sum0_done, rcp0_done, prob0_done, p0l_ready = sem("sum0_done"), sem("rcp0_done"), sem("prob0_done"), sem("p0l_ready")
        prob_done, xl_ready = sem("prob_done"), sem("xl_ready")
        rs_done, gamma_done, beta_done = sem("rs_done"), sem("gamma_done"), sem("beta_done")

        def units(i, k):
            return TURN * i + k

        def tiles(i, k, t):
            return TILES * TURN * i + TILES * k + t

        def chunks(i, k, c):
            return KC * TURN * i + KC * k + c

        def blocks(i, b):
            return 2 * i + b

        def wait(eng, semaphore, count):
            if not (type(count) is int and count <= 0):
                eng.wait_ge(semaphore, count)

        def unit_exists(i, k):
            return type(i) is not int or 0 <= k < UNITS

        def block_exists(i, b):
            return type(i) is not int or 0 <= b < BLOCKS

        def run(eng, step):
            for k in range(FIRST):
                step(0, k)
            with eng.Fori(0, TURNS) as i:
                for k in range(FIRST, FIRST + TURN):
                    step(i, k)
            for k in range(LOOP_END, STEPS):
                step(0, k)

        def part3(a_h, a_l, b_h, b_l):
            return ((a_h, b_h), (a_l, b_h), (a_h, b_l))

        def f32(ap):
            return ap.bitcast(F32)

        def wide(ap, n):
            return ap.unsqueeze(2).to_broadcast([ap.shape[0], ap.shape[1], n])

        block = ctx.enter_context(nc.Block())

        @block.sync
        def _(sp):
            sp.dma_start(ctxT_sb[:], ctxT.rearrange("(c p) k -> p c k", p=P)).then_inc(ld_ctx, 16)
            sp.dma_start(raw0[:], w0k.rearrange("(c p) e -> p c e", p=P)).then_inc(ld_w0k, 16)
            sp.dma_start(raw1[:], w0q.rearrange("(c p) e -> p c e", p=P)).then_inc(ld_w0q, 16)
            sp.dma_start(x_raw[:].rearrange("p c t -> p (c t)"), xT[0, 0]).then_inc(ld_xT, 16)
            sp.dma_start(raw3[:], w0v.rearrange("(c p) e -> p c e", p=P)).then_inc(ld_w0v, 16)
            sp.dma_start(raw2[:], w1q.rearrange("(c p) e -> p c e", p=P)).then_inc(ld_w1q, 16)
            sp.wait_ge(mm_k0T, 2)
            sp.dma_start(raw0[:], w1k.rearrange("(c p) e -> p c e", p=P)).then_inc(ld_w1k, 16)
            sp.wait_ge(mm_a0, 2)
            sp.dma_start(raw1[:], w1v.rearrange("(c p) e -> p c e", p=P)).then_inc(ld_w1v, 16)
            sp.wait_ge(mm_v0T, 2)
            sp.dma_start(raw3[:], w1o.rearrange("(c p) e -> p c e", p=P)).then_inc(ld_w1o, 16)
            sp.wait_ge(vd_zero, 2)
            sp.wait_ge(v1_h_ready, BATCH)
            sp.wait_ge(v1_ready, BATCH)
            for part, blocks_of in ((v1_h, vd_h), (v1_l, vd_l)):
                for c in range(KC):
                    done = KSTART[c] if c == 0 else KSTART[c - 1] + KROWS
                    while done < KSTART[c] + KROWS:
                        head, key = divmod(done, KEYS)
                        m = min(KEYS - key, KSTART[c] + KROWS - done)
                        r = done - KSTART[c]
                        own = slice(head * HEAD_DIM, (head + 1) * HEAD_DIM)
                        sp.dma_start(
                            f32(blocks_of[r:r + m]).rearrange("r b g c d -> r (b g) c d")[:, :, c, own],
                            f32(part[key:key + m]).rearrange("r b (g d) -> r (b g) d", d=P)[:, :, own],
                        ).then_inc(vd_placed, 16)
                        done += m

            def next_inputs(i, b):
                if not block_exists(i, b + 1):
                    return
                j = i + (b + 1) // 2
                wait(sp, xl_ready, CH * blocks(i, b + 1))
                wait(sp, sel0_done, blocks(i, b + 1))
                sp.dma_start(x_raw[:].rearrange("p c t -> p (c t)"), xT[(b + 1) % 2, j]).then_inc(ld_xT, 16)
                sp.dma_start(mask_sb[:].rearrange("p t k -> p (t k)"), mask[(b + 1) % 2, j]).then_inc(ld_mask, 16)

            def load_rows(i, b, t):
                if not block_exists(i, b):
                    return
                wait(sp, stored[t], 16 * blocks(i, b))
                sp.dma_start(y[:, t, :], x[b % 2, TILES * (i + b // 2) + t]).then_inc(ld_x[t], 16)

            def store(i, b):
                if not block_exists(i, b):
                    return
                for t in range(TILES):
                    wait(sp, beta_done, TILES * blocks(i, b) + t + 1)
                    sp.dma_start(out[b % 2, i + b // 2, t], y[:, t, :]).then_inc(stored[t], 16)
                    if t > 0:
                        load_rows(i, b + 1, t - 1)
                load_rows(i, b + 1, TILES - 1)

            next_inputs(0, 0)
            sp.wait_ge(v0_ready, BATCH)
            sp.wait_ge(mm_v1T, 2)
            for t in range(TILES):
                load_rows(0, 0, t)
            next_inputs(0, 1)
            with sp.Fori(0, SP_TURNS) as i:
                for b in (2, 3):
                    next_inputs(i, b)
                    store(i, b - 2)
            for b in range(2 + 2 * SP_TURNS, BLOCKS + 2):
                next_inputs(0, b)
                store(0, b - 2)
            for t in range(TILES):
                sp.wait_ge(stored[t], 16 * BLOCKS)

        @block.gpsimd
        def _(pool):
            def x_rest(i, b, c):
                if not block_exists(i, b):
                    return
                wait(pool, xh_ready, CH * blocks(i, b) + c + 1)
                nc.gpsimd.tensor_tensor(x_l[:, c], x_raw[:, c], f32(x_h[:, c]), ALU.subtract).then_inc(xl_ready, 1)

            nc.gpsimd.memset(ident[:], 0.0).then_inc(ident_zero, 1)
            pool.wait_ge(ident_zero, 1)
            nc.gpsimd.affine_select(out=ident[:], in_=ident[:], compare_op=ALU.not_equal, fill=1.0, base=0,
                                    pattern=[[-1, P]], channel_multiplier=1).then_inc(ident_ready, 1)
            nc.gpsimd.memset(minus_half[:], -0.5).then_inc(const_ready, 1)
            for part in (kd_h, kd_l):
                nc.gpsimd.memset(f32(part[:]), 0.0).then_inc(kd_zero, 1)
            for c in range(CH):
                x_rest(0, 0, c)
            for part in (vd_h, vd_l):
                nc.gpsimd.memset(f32(part[:]), 0.0).then_inc(vd_zero, 1)
            for c in range(CH):
                pool.wait_ge(wo_h_ready, c + 1)
                nc.gpsimd.tensor_tensor(wo_l[:, c], raw3[:, c], f32(wo_h[:, c]), ALU.subtract).then_inc(wo_ready, 1)

            def scale_probs(i, k, t):
                if not unit_exists(i, k):
                    return
                wait(pool, rcp_done, tiles(i, k, t) + 1)
                ap = prob[:, k % 2, t].rearrange("p (h k) -> p h k", k=KEYS)
                nc.gpsimd.tensor_tensor(ap, ap, wide(rc[:, k % 2, t], KEYS), ALU.mult).then_inc(prob_done, 1)

            def root(i, b, h):
                if not block_exists(i, b):
                    return
                own = slice(2 * h, 2 * h + 2)
                wait(pool, var_done, 2 * blocks(i, b) + h + 1)
                nc.gpsimd.tensor_tensor(rs[:, own], ve[:, own], minus_half[:, own], ALU.pow).then_inc(rs_done, 1)

            def affine(i, b, t):
                if not block_exists(i, b):
                    return
                m = TILES * blocks(i, b) + t
                wait(pool, z_done, m + 1)
                nc.gpsimd.tensor_tensor(y[:, t], y[:, t], rows_sb[:, 0], ALU.mult).then_inc(gamma_done, 1)
                wait(pool, gamma_done, m + 1)
                nc.gpsimd.tensor_tensor(y[:, t], y[:, t], rows_sb[:, 1], ALU.add).then_inc(beta_done, 1)

            def step(i, k):
                g, b = k % CH, k // CH
                scale_probs(i, k - 1, 3)
                if g == 3:
                    x_rest(i, b + 1, 0)
                    x_rest(i, b + 1, 1)
                if g == 0:
                    affine(i, b - 2, 0)
                scale_probs(i, k, 0)
                if g == 3:
                    x_rest(i, b + 1, 2)
                    x_rest(i, b + 1, 3)
                if g == 0:
                    root(i, b - 2, 1)
                if g == 1:
                    affine(i, b - 2, 2)
                scale_probs(i, k, 1)
                if g == 3:
                    root(i, b - 1, 0)
                if g == 0:
                    affine(i, b - 2, 1)
                scale_probs(i, k, 2)
                if g == 1:
                    affine(i, b - 2, 3)

            pool.wait_ge(ld_rows, 16)
            pool.wait_ge(const_ready, 1)
            run(pool, step)

        @block.scalar
        def _(act):
            act.dma_start(cols_sb[:].rearrange("p a c -> p (a c)"), cols).then_inc(ld_cols, 16)
            act.dma_start(mask_sb[:].rearrange("p t k -> p (t k)"), mask[0, 0]).then_inc(ld_mask, 16)
            flat = rows.rearrange("(o n) -> o n", o=1)
            act.dma_start(bo_sb[:], flat[:, 2 * DIM:3 * DIM].to_broadcast([P, DIM])).then_inc(ld_bo, 16)
            act.dma_start(rows_sb[:].rearrange("p a d -> p (a d)"),
                          flat[:, 0:2 * DIM].to_broadcast([P, 2 * DIM])).then_inc(ld_rows, 16)

            def leave(banks, made, to, bias, ready, scale=1.0):
                for c in range(CH):
                    act.wait_ge(made, c // 2 + 1)
                    src = banks[c // 2][:, 0:2 * BATCH * KEYS].rearrange("p (e k) -> p e k", e=2)[:, c % 2]
                    nc.scalar.activation(to[:, c], src, ACT.Identity, bias=bias[:, c:c + 1], scale=scale).then_inc(ready, 1)

            def round_x(i, b, first, last):
                if not block_exists(i, b):
                    return
                wait(act, ld_xT, 16 * (blocks(i, b) + 1))
                wait(act, q_done, CH * blocks(i, b))
                for c in range(first, last):
                    nc.scalar.activation(x_h[:, c], x_raw[:, c], ACT.Copy).then_inc(xh_ready, 1)

            def exp0(i, b):
                if not block_exists(i, b):
                    return
                wait(act, sub0_done, blocks(i, b) + 1)
                wait(act, p0t_done, blocks(i, b))
                nc.scalar.activation(e0[:], m0[:], ACT.Exp).then_inc(exp0_done, 1)

            def round_p0(i, b):
                if not block_exists(i, b):
                    return
                wait(act, p0t_done, blocks(i, b) + 1)
                nc.scalar.activation(p0_h[:, b % 2], ps_0[0:KEYS, :], ACT.Copy).then_inc(p0h_ready, 1)

            def round_q(i, k):
                if not unit_exists(i, k):
                    return
                wait(act, q_done, units(i, k) + 1)
                nc.scalar.activation(q_h[:, k % 2], ps_q[:], ACT.Identity,
                                     bias=cols_sb[:, 3, k % CH:k % CH + 1]).then_inc(qh_ready, 1)

            act.wait_ge(ld_cols, 16)
            leave(bank[1:3], mm_k0T, k0T, cols_sb[:, 1], k0T_ready)
            round_x(0, 0, 0, CH)
            leave(bank[5:7], mm_v0T, v0T, cols_sb[:, 2], v0T_ready)
            exp0(0, 0)
            act.wait_ge(ld_w1q, 16)
            for c in range(CH):
                nc.scalar.activation(wq_h[:, c], raw2[:, c], ACT.Copy).then_inc(wq_h_ready, 1)
            for b in range(BATCH):
                act.wait_ge(mm_u, b + 1)
                nc.scalar.activation(u_h[:, b], bank[1 + b][0:KEYS, :], ACT.Copy).then_inc(u_h_ready, 1)
            act.wait_ge(bk1_ready, 1)
            leave(bank[5:7], mm_k1T, k1T, bk1_scaled, k1T_ready, scale=SCALE)
            leave(bank[3:5], mm_v1T, v1T, cols_sb[:, 5], v1T_ready)
            round_p0(0, 0)
            for b in range(BATCH):
                act.wait_ge(mm_v1, b + 1)
                nc.scalar.activation(v1_h[:, b], bank[5 + b][0:KEYS, :], ACT.Copy).then_inc(v1_h_ready, 1)
            round_q(0, 0)
            act.wait_ge(ld_w1o, 16)
            for c in range(CH):
                nc.scalar.activation(wo_h[:, c], raw3[:, c], ACT.Copy).then_inc(wo_h_ready, 1)

            def exps(i, k, t):
                if not unit_exists(i, k):
                    return
                wait(act, max_done, tiles(i, k, t) + 1)
                for h in range(GROUP_HEADS):
                    own = slice(h * KEYS, (h + 1) * KEYS)
                    e = nc.scalar.activation(prob[:, k % 2, t, own], ps_s[t % 2][:, own], ACT.Exp, bias=mx[:, k % 2, t, h:h + 1])
                e.then_inc(exp_done, 1)

            def round_pt(i, k, c):
                if not unit_exists(i, k):
                    return
                if type(i) is int and k == 0 and c == 0:
                    act.wait_ge(vd_placed, 16 * 12)
                wait(act, t_done, chunks(i, k, c) + 1)
                nc.scalar.activation(pt_h[:, c], ps_t[c % 2][0:KROWS, :], ACT.Copy).then_inc(pth_ready, 1)

            def round_ct(i, k):
                if not unit_exists(i, k):
                    return
                wait(act, pv_done, units(i, k) + 1)
                nc.scalar.activation(ct_h[:, k // CH % 2, k % CH], ps_pv[:], ACT.Copy).then_inc(cth_ready, 1)

            def normalise(i, b, t):
                if not block_exists(i, b):
                    return
                wait(act, nb_done, 2 * blocks(i, b) + t // 2 + 1)
                nc.scalar.activation(y[:, t], y[:, t], ACT.Identity, bias=nb[:, t:t + 1],
                                     scale=rs[:, t:t + 1]).then_inc(z_done, 1)

            def step(i, k):
                g, b = k % CH, k // CH
                round_pt(i, k - 2, 2)
                exps(i, k, 0)
                if g == 0:
                    normalise(i, b - 2, 1)
                if g == 3:
                    round_p0(i, b + 1)
                if g == 1:
                    normalise(i, b - 2, 2)
                exps(i, k, 1)
                round_ct(i, k - 2)
                if g == 1:
                    normalise(i, b - 2, 3)
                    exp0(i, b + 1)
                round_pt(i, k - 1, 0)
                exps(i, k, 2)
                round_q(i, k + 1)
                round_pt(i, k - 1, 1)
                if g == 2:
                    round_x(i, b + 1, 0, 2)
                exps(i, k, 3)
                if g == 2:
                    round_x(i, b + 1, 2, CH)
                if g == 3:
                    normalise(i, b - 1, 0)

            run(act, step)

        @block.vector
        def _(dve):
            def layer0_scores(i, b):
                if not block_exists(i, b):
                    return
                n = blocks(i, b)
                v = slice(b % 2 * KEYS, (b % 2 + 1) * KEYS)
                wait(dve, l0_done, n + 1)
                nc.vector.tensor_tensor(m0[:], ps_0[:, 0:TILES * KEYS].rearrange("p (t k) -> p t k", k=KEYS),
                                        c0[:, v].unsqueeze(1).to_broadcast([P, TILES, KEYS]), ALU.add).then_inc(add0_done, 1)
                wait(dve, ld_mask, 16 * (n + 1))
                nc.vector.tensor_scalar(n0[:], mask_sb[:], 0.0, NEG, ALU.is_equal, ALU.mult).then_inc(neg0_done, 1)
                wait(dve, add0_done, n + 1)
                wait(dve, neg0_done, n + 1)
                nc.vector.scalar_tensor_tensor(out=m0[:], in0=n0[:], scalar=0.0, in1=m0[:],
                                               op0=ALU.is_equal, op1=ALU.mult).then_inc(kept0_done, 1)
                wait(dve, kept0_done, n + 1)
                nc.vector.tensor_tensor(m0[:], m0[:], n0[:], ALU.add).then_inc(sel0_done, 1)
                wait(dve, sel0_done, n + 1)
                nc.vector.reduce_max(stat0[:, 0], m0[:], AX_X).then_inc(max0_done, 1)
                wait(dve, max0_done, n + 1)
                nc.vector.tensor_tensor(m0[:], m0[:], wide(stat0[:, 0], KEYS), ALU.subtract).then_inc(sub0_done, 1)

            def layer0_probs(i, b):
                if not block_exists(i, b):
                    return
                n = blocks(i, b)
                wait(dve, exp0_done, n + 1)
                nc.vector.reduce_sum(stat0[:, 1], e0[:], AX_X).then_inc(sum0_done, 1)
                wait(dve, sum0_done, n + 1)
                nc.vector.reciprocal(stat0[:, 2], stat0[:, 1]).then_inc(rcp0_done, 1)
                wait(dve, rcp0_done, n + 1)
                nc.vector.tensor_tensor(e0[:], e0[:], wide(stat0[:, 2], KEYS), ALU.mult).then_inc(prob0_done, 1)

            def p0_rest(i, b):
                if not block_exists(i, b):
                    return
                wait(dve, p0h_ready, blocks(i, b) + 1)
                nc.vector.tensor_tensor(p0_l[:, b % 2], ps_0[0:KEYS, :], f32(p0_h[:, b % 2]),
                                        ALU.subtract).then_inc(p0l_ready, 1)

            def q_rest(i, k):
                if not unit_exists(i, k):
                    return
                wait(dve, qh_ready, units(i, k) + 1)
                nc.vector.scalar_tensor_tensor(out=q_l[:, k % 2], in0=ps_q[:], scalar=cols_sb[:, 3, k % CH:k % CH + 1],
                                               in1=f32(q_h[:, k % 2]), op0=ALU.add, op1=ALU.subtract).then_inc(ql_ready, 1)

            dve.wait_ge(ld_cols, 16)
            nc.vector.tensor_copy(bq0_wide[:], wide(cols_sb[:, 0], P)).then_inc(bq0_ready, 1)
            nc.vector.tensor_scalar(bk1_scaled[:], cols_sb[:, 4], SCALE, None, ALU.mult).then_inc(bk1_ready, 1)
            for h in range(2):
                dve.wait_ge(mm_a0, h + 1)
                nc.vector.tensor_copy(a0[:, 2 * h:2 * h + 2].rearrange("p c k -> p (c k)"),
                                      bank[3 + h][:, 0:2 * BATCH * KEYS]).then_inc(a0_ready, 1)
            dve.wait_ge(mm_c0, 1)
            nc.vector.tensor_copy(c0[:], ps_0[:, 0:BATCH * KEYS]).then_inc(c0_ready, 1)
            dve.wait_ge(c0_ready, 1)
            layer0_scores(0, 0)
            for c in range(CH):
                dve.wait_ge(wq_h_ready, c + 1)
                nc.vector.tensor_tensor(wq_l[:, c], raw2[:, c], f32(wq_h[:, c]), ALU.subtract).then_inc(wq_ready, 1)
            layer0_probs(0, 0)
            dve.wait_ge(ld_bo, 16)
            for b in range(BATCH):
                dve.wait_ge(mm_v0, b + 1)
                nc.vector.tensor_tensor(v0o[:, b], bank[3 + b][0:KEYS, :], bo_sb[0:KEYS], ALU.add).then_inc(v0o_ready, 1)
            for b in range(BATCH):
                dve.wait_ge(u_h_ready, b + 1)
                nc.vector.tensor_tensor(u_l[:, b], bank[1 + b][0:KEYS, :], f32(u_h[:, b]), ALU.subtract).then_inc(u_ready, 1)
            for b in range(BATCH):
                dve.wait_ge(v0o_ready, b + 1)
                nc.vector.tensor_copy(v0_h[:, b], v0o[:, b]).then_inc(v0_h_ready, 1)
            for b in range(BATCH):
                dve.wait_ge(v0_h_ready, b + 1)
                nc.vector.tensor_tensor(v0_l[:, b], v0o[:, b], f32(v0_h[:, b]), ALU.subtract).then_inc(v0_ready, 1)
            dve.wait_ge(kd_zero, 2)
            dve.wait_ge(k1T_ready, CH)
            for h in range(GROUP_HEADS):
                own, at = slice(h * HEAD_DIM, (h + 1) * HEAD_DIM), slice(h * KEYS, (h + 1) * KEYS)
                nc.vector.tensor_copy(kd_h[own, :, :, at],
                                      k1T[own].rearrange("p c (b k) -> p b c k", b=BATCH)).then_inc(kd_h_ready, 1)
            for h in range(GROUP_HEADS):
                own, at = slice(h * HEAD_DIM, (h + 1) * HEAD_DIM), slice(h * KEYS, (h + 1) * KEYS)
                dve.wait_ge(kd_h_ready, h + 1)
                nc.vector.tensor_tensor(kd_l[own, :, :, at], k1T[own].rearrange("p c (b k) -> p b c k", b=BATCH),
                                        f32(kd_h[own, :, :, at]), ALU.subtract).then_inc(kd_ready, 1)
            p0_rest(0, 0)
            for b in range(BATCH):
                dve.wait_ge(v1_h_ready, b + 1)
                nc.vector.tensor_tensor(v1_l[:, b], bank[5 + b][0:KEYS, :], f32(v1_h[:, b]), ALU.subtract).then_inc(v1_ready, 1)
            q_rest(0, 0)

            def softmax_part(i, k, t):
                pk, pt = (k, t - 1) if t > 0 else (k - 1, TILES - 1)
                if unit_exists(i, k):
                    wait(dve, s_done, tiles(i, k, t) + 1)
                    nc.vector.reduce_max(mx[:, k % 2, t], ps_s[t % 2][:, 0:GCOLS].rearrange("p (h k) -> p h k", k=KEYS),
                                         AX_X, negate=True).then_inc(max_done, 1)
                if unit_exists(i, pk):
                    wait(dve, exp_done, tiles(i, pk, pt) + 1)
                    nc.vector.reduce_sum(sm[:, pk % 2, pt], prob[:, pk % 2, pt].rearrange("p (h k) -> p h k", k=KEYS),
                                         AX_X).then_inc(sum_done, 1)
                    wait(dve, sum_done, tiles(i, pk, pt) + 1)
                    nc.vector.reciprocal(rc[:, pk % 2, pt], sm[:, pk % 2, pt]).then_inc(rcp_done, 1)

            def pt_rest(i, k, c):
                if not unit_exists(i, k):
                    return
                wait(dve, pth_ready, chunks(i, k, c) + 1)
                nc.vector.tensor_tensor(pt_l[:, c], ps_t[c % 2][0:KROWS, :], f32(pt_h[:, c]),
                                        ALU.subtract).then_inc(ptl_ready, 1)

            def ct_rest(i, k):
                if not unit_exists(i, k):
                    return
                wait(dve, cth_ready, units(i, k) + 1)
                nc.vector.tensor_tensor(ct_l[:, k // CH % 2, k % CH], ps_pv[:], f32(ct_h[:, k // CH % 2, k % CH]),
                                        ALU.subtract).then_inc(ctl_ready, 1)

            def residual(i, b, t):
                if not block_exists(i, b):
                    return
                m = TILES * blocks(i, b) + t
                wait(dve, out_done, m + 1)
                wait(dve, ld_x[t], 16 * (blocks(i, b) + 1))
                nc.vector.tensor_tensor(y[:, t], ps_out[:], y[:, t], ALU.add).then_inc(y_done, 1)
                wait(dve, y_done, m + 1)
                nc.vector.bn_stats(bn6[:, t], y[:, t]).then_inc(bn_done, 1)

            def variance(i, b, h):
                if not block_exists(i, b):
                    return
                n, own = 2 * blocks(i, b) + h, slice(2 * h, 2 * h + 2)
                wait(dve, bn_done, 2 * (n + 1))
                nc.vector.tensor_tensor(both[:, own], bn6[:, own, 0:3], bn6[:, own, 3:6], ALU.add).then_inc(both_done, 1)
                nc.vector.tensor_tensor(diff[:, own], bn6[:, own, 1], bn6[:, own, 4], ALU.subtract).then_inc(diff_done, 1)
                wait(dve, both_done, n + 1)
                nc.vector.tensor_scalar(within[:, own], both[:, own, 2], 1.0 / DIM, LN_EPS,
                                        ALU.mult, ALU.add).then_inc(within_done, 1)
                wait(dve, diff_done, n + 1)
                nc.vector.scalar_tensor_tensor(out=between[:, own], in0=diff[:, own], scalar=0.25, in1=diff[:, own],
                                               op0=ALU.mult, op1=ALU.mult).then_inc(between_done, 1)
                wait(dve, within_done, n + 1)
                wait(dve, between_done, n + 1)
                nc.vector.tensor_tensor(ve[:, own], within[:, own], between[:, own], ALU.add).then_inc(var_done, 1)

            def offset(i, b, h):
                if not block_exists(i, b):
                    return
                own = slice(2 * h, 2 * h + 2)
                wait(dve, rs_done, 2 * blocks(i, b) + h + 1)
                nc.vector.scalar_tensor_tensor(out=nb[:, own], in0=both[:, own, 1], scalar=-0.5, in1=rs[:, own],
                                               op0=ALU.mult, op1=ALU.mult).then_inc(nb_done, 1)

            def step(i, k):
                g, b = k % CH, k // CH
                softmax_part(i, k, 0)
                if g == 0:
                    variance(i, b - 2, 1)
                pt_rest(i, k - 2, 2)
                if g == 1:
                    layer0_scores(i, b + 1)
                softmax_part(i, k, 1)
                if g == 2:
                    residual(i, b - 1, 1)
                if g == 3:
                    p0_rest(i, b + 1)
                softmax_part(i, k, 2)
                ct_rest(i, k - 2)
                pt_rest(i, k - 1, 0)
                if g == 0:
                    offset(i, b - 2, 1)
                if g == 1:
                    layer0_probs(i, b + 1)
                if g == 2:
                    variance(i, b - 1, 0)
                if g == 3:
                    offset(i, b - 1, 0)
                softmax_part(i, k, 3)
                if g == 1:
                    residual(i, b - 1, 0)
                if g == 2:
                    residual(i, b - 1, 2)
                q_rest(i, k + 1)
                pt_rest(i, k - 1, 1)
                if g == 3:
                    residual(i, b - 1, 3)

            run(dve, step)

        @block.tensor
        def _(pe):
            def project(banks, weights, moving, made):
                for e in range(CH):
                    for c in range(CH):
                        mm = nc.tensor.matmul(banks[e // 2][:, (e % 2) * BATCH * KEYS:(e % 2 + 1) * BATCH * KEYS],
                                              weights[:, c, e * P:(e + 1) * P], moving[:, c],
                                              start=(c == 0), stop=(c == CH - 1))
                    if e % 2:
                        mm.then_inc(made, 1)

            def to_rows(banks, src, made):
                for b in range(BATCH):
                    for e in range(CH):
                        mm = nc.tensor.transpose(banks[b][0:KEYS, e * P:(e + 1) * P],
                                                 src[:, e, b * KEYS:(b + 1) * KEYS], ident[:])
                    mm.then_inc(made, 1)

            def layer0(i, b, t):
                if not block_exists(i, b):
                    return
                if t == 0:
                    wait(pe, ld_xT, 16 * (blocks(i, b) + 1))
                    wait(pe, p0l_ready, blocks(i, b))
                for c in range(CH):
                    mm = nc.tensor.matmul(ps_0[:, t * KEYS:(t + 1) * KEYS], x_raw[:, c, t * P:(t + 1) * P],
                                          a0[:, c, b % 2 * KEYS:(b % 2 + 1) * KEYS],
                                          start=(c == 0), stop=(c == CH - 1))
                if t == TILES - 1:
                    mm.then_inc(l0_done, 1)

            def transpose0(i, b):
                if not block_exists(i, b):
                    return
                wait(pe, prob0_done, blocks(i, b) + 1)
                for t in range(TILES):
                    mm = nc.tensor.transpose(ps_0[0:KEYS, t * P:(t + 1) * P], e0[:, t], ident[:])
                mm.then_inc(p0t_done, 1)

            def query(i, k, first, last):
                if not unit_exists(i, k):
                    return
                b, g = k // CH, k % CH
                own = slice(g * P, (g + 1) * P)
                if first == 0:
                    wait(pe, ql_ready, units(i, k))
                for m in range(first, last):
                    if m < 2 * CH:
                        c = m // 2
                        if g == 0 and m % 2 == 0:
                            wait(pe, xh_ready, CH * blocks(i, b) + c + 1)
                        w, v = (wq_h, wq_l)[m % 2][:, c, own], x_h[:, c]
                    elif m < 3 * CH:
                        c = m - 2 * CH
                        if g == 0:
                            wait(pe, xl_ready, CH * blocks(i, b) + c + 1)
                        w, v = wq_h[:, c, own], x_l[:, c]
                    else:
                        if g == 0 and m == 3 * CH:
                            wait(pe, p0l_ready, blocks(i, b) + 1)
                        w, v = part3(u_h[:, b % 2, own], u_l[:, b % 2, own], p0_h[:, b % 2], p0_l[:, b % 2])[m - 3 * CH]
                    mm = nc.tensor.matmul(ps_q[:], w, v, start=(m == 0), stop=(m == 3 * CH + 2))
                if last == 3 * CH + 3:
                    mm.then_inc(q_done, 1)

            def scores(i, k, t):
                if not unit_exists(i, k):
                    return
                b, g = k // CH, k % CH
                if t == 0:
                    wait(pe, ql_ready, units(i, k) + 1)
                wait(pe, exp_done, tiles(i, k, t) - 1)
                own = slice(t * P, (t + 1) * P)
                for m, (w, v) in enumerate(part3(q_h[:, k % 2, own], q_l[:, k % 2, own], kd_h[:, b % 2, g], kd_l[:, b % 2, g])):
                    mm = nc.tensor.matmul(ps_s[t % 2][:, 0:GCOLS], w, v, start=(m == 0), stop=(m == 2))
                mm.then_inc(s_done, 1)

            def transposes(i, k, c):
                if not unit_exists(i, k):
                    return
                if c == 0:
                    wait(pe, prob_done, tiles(i, k, TILES))
                wait(pe, ptl_ready, chunks(i, k, c) - (0, 2, 1)[c])
                for t in range(TILES):
                    mm = nc.tensor.transpose(ps_t[c % 2][0:KROWS, t * P:(t + 1) * P],
                                             prob[:, k % 2, t, KSTART[c]:KSTART[c] + KROWS], ident[:])
                mm.then_inc(t_done, 1)

            def context(i, k, c):
                if not unit_exists(i, k):
                    return
                b, g = k // CH, k % CH
                if c == 0:
                    wait(pe, ctl_ready, units(i, k))
                wait(pe, ptl_ready, chunks(i, k, c) + 1)
                for m, (w, v) in enumerate(part3(vd_h[:, b % 2, g, c], vd_l[:, b % 2, g, c], pt_h[:, c], pt_l[:, c])):
                    mm = nc.tensor.matmul(ps_pv[:], w, v, start=(c == 0 and m == 0), stop=(c == KC - 1 and m == 2))
                if c == KC - 1:
                    mm.then_inc(pv_done, 1)

            def output(i, b, first, last):
                if not block_exists(i, b):
                    return
                for n in range(first, last):
                    t, m = divmod(n, 3 * CH + 3)
                    own = slice(t * P, (t + 1) * P)
                    if m == 0:
                        wait(pe, y_done, TILES * blocks(i, b) + t)
                    if m < 3:
                        w, v = part3(p0_h[:, b % 2, own], p0_l[:, b % 2, own], v0_h[:, b % 2], v0_l[:, b % 2])[m]
                    else:
                        c = m // 3 - 1
                        if t == 0 and m == 3 * CH:
                            wait(pe, ctl_ready, CH * (blocks(i, b) + 1))
                        w, v = part3(ct_h[:, b % 2, c, own], ct_l[:, b % 2, c, own], wo_h[:, c], wo_l[:, c])[m % 3]
                    mm = nc.tensor.matmul(ps_out[:], w, v, start=(m == 0), stop=(m == 3 * CH + 2))
                    if m == 3 * CH + 2:
                        mm.then_inc(out_done, 1)

            pe.wait_ge(ld_ctx, 16)
            pe.wait_ge(ld_w0k, 16)
            project(bank[1:3], raw0, ctxT_sb, mm_k0T)
            pe.wait_ge(ld_w0q, 16)
            pe.wait_ge(k0T_ready, CH)
            project(bank[3:5], raw1, k0T, mm_a0)
            pe.wait_ge(bq0_ready, 1)
            for c in range(CH):
                mm = nc.tensor.matmul(ps_0[:, 0:BATCH * KEYS], bq0_wide[:, c], k0T[:, c], start=(c == 0), stop=(c == CH - 1))
            mm.then_inc(mm_c0, 1)
            pe.wait_ge(ld_w0v, 16)
            project(bank[5:7], raw3, ctxT_sb, mm_v0T)
            pe.wait_ge(a0_ready, 2)
            pe.wait_ge(c0_ready, 1)
            for t in range(TILES):
                layer0(0, 0, t)
            pe.wait_ge(v0T_ready, CH)
            pe.wait_ge(ident_ready, 1)
            to_rows(bank[3:5], v0T, mm_v0)
            pe.wait_ge(ld_w1q, 16)
            for b in range(BATCH):
                for c in range(CH):
                    mm = nc.tensor.matmul(bank[1 + b][0:KEYS, :], v0T[:, c, b * KEYS:(b + 1) * KEYS], raw2[:, c],
                                          start=(c == 0), stop=(c == CH - 1))
                mm.then_inc(mm_u, 1)
            pe.wait_ge(ld_w1k, 16)
            project(bank[5:7], raw0, ctxT_sb, mm_k1T)
            transpose0(0, 0)
            pe.wait_ge(v0o_ready, BATCH)
            pe.wait_ge(ld_w1v, 16)
            project(bank[3:5], raw1, ctxT_sb, mm_v1T)
            pe.wait_ge(wq_ready, CH)
            pe.wait_ge(u_ready, BATCH)
            query(0, 0, 0, 3 * CH + 3)
            pe.wait_ge(k1T_ready, CH)
            pe.wait_ge(v1T_ready, CH)
            to_rows(bank[5:7], v1T, mm_v1)
            pe.wait_ge(kd_ready, GROUP_HEADS)

            def step(i, k):
                g, b = k % CH, k // CH

                def part(t):
                    if g == 0:
                        layer0(i, b + 1, t)
                    else:
                        s = TILES * (g - 1) + t
                        output(i, b - 1, sum(OUT_SHARE[:s]), sum(OUT_SHARE[:s + 1]))

                scores(i, k, 0)
                query(i, k + 1, 0, 5)
                context(i, k - 2, 1)
                part(0)
                scores(i, k, 1)
                context(i, k - 2, 2)
                query(i, k + 1, 5, 10)
                transposes(i, k - 1, 0)
                part(1)
                scores(i, k, 2)
                query(i, k + 1, 10, 15)
                transposes(i, k - 1, 1)
                part(2)
                scores(i, k, 3)
                transposes(i, k - 1, 2)
                if type(i) is int and k == 1:
                    pe.wait_ge(vd_placed, 16 * 12)
                    pe.wait_ge(v0_ready, BATCH)
                context(i, k - 1, 0)
                part(3)
                if g == 2:
                    transpose0(i, b + 1)

            run(pe, step)


def kernel(**inputs):
    import numpy as np
    import concourse.bacc as bacc
    from concourse.bass_utils import run_bass_kernel_spmd

    def arr(name):
        return np.asarray(inputs[name])

    x, ctx, mask = arr("x"), arr("ctx_1024"), arr("mask_BxSxS2_ik0")
    w_qkv, b_qkv = arr("L1_xattn_W_qkv"), arr("L1_xattn_b_qkv")
    nj = SEQ // BLOCK
    by_channel = [arr("L0_xattn_bq"), arr("L0_xattn_bk"), arr("L0_xattn_bv"), b_qkv[:DIM], b_qkv[DIM:2 * DIM], b_qkv[2 * DIM:]]
    arrays = {
        "xT": x.reshape(BATCH, nj, BLOCK, CH, P).transpose(0, 1, 4, 3, 2).reshape(BATCH, nj, P, CH * BLOCK),
        "x": x,
        "mask": mask.reshape(BATCH, nj, TILES, P, KEYS).transpose(0, 1, 3, 2, 4).reshape(BATCH, nj, P, TILES * KEYS),
        "ctxT": ctx.reshape(BATCH * KEYS, DIM).T,
        "w0k": arr("L0_xattn_Wk").T, "w0q": arr("L0_xattn_Wq"), "w0v": arr("L0_xattn_Wv").T,
        "w1q": w_qkv[:DIM].T, "w1k": w_qkv[DIM:2 * DIM].T, "w1v": w_qkv[2 * DIM:].T, "w1o": arr("L1_xattn_W_o").T,
        "cols": np.stack(by_channel).reshape(6, CH, P).transpose(2, 0, 1).reshape(P, 6 * CH),
        "rows": np.concatenate([arr("L1_xattn_ln_gamma"), arr("L1_xattn_ln_beta"), arr("L1_xattn_b_o")]),
    }
    arrays = {"in_" + n: np.ascontiguousarray(a) for n, a in arrays.items()}
    nc = bacc.Bacc("TRN2", target_bir_lowering=False, num_devices=1)
    aps = {n[3:]: nc.dram_tensor(n, a.shape, mybir.dt.from_np(a.dtype), kind="ExternalInput").ap() for n, a in arrays.items()}
    out = nc.dram_tensor("out_0", (BATCH, SEQ, DIM), F32, kind="ExternalOutput").ap()
    aps["x"] = aps["x"].rearrange("b (n p) d -> b n p d", p=P)
    xattn_kernel(nc, **aps, out=out.rearrange("b (j t p) d -> b j t p d", t=TILES, p=P))
    r = run_bass_kernel_spmd(nc, [arrays], core_ids=[0])
    return r.results[0]["out_0"]
```

```python
from contextlib import ExitStack

import concourse.bass as bass
from concourse import mybir

F32 = mybir.dt.float32
F32R = mybir.dt.float32r
I32 = mybir.dt.int32
ALU = mybir.AluOpType
ACT = mybir.ActivationFunctionType
AX_X = mybir.AxisListType.X

BATCH, SEQ, DIM, KEYS = 2, 2048, 512, 77
HEADS = 16
HEAD_DIM = DIM // HEADS
P = 128
CH = DIM // P
GROUP_HEADS = P // HEAD_DIM
TILES = 4
BLOCK = TILES * P
BLOCKS = BATCH * SEQ // BLOCK
UNITS = BLOCKS * CH
GCOLS = GROUP_HEADS * KEYS
KC = 3
KROWS = -(-GCOLS // KC)
KSTART = [min(c * KROWS, GCOLS - KROWS) for c in range(KC)]
TAIL = P - KEYS
REST = KEYS - TAIL
BROWS = REST + KEYS
QUERY = OUTPUT = 3 * CH + 2
NEG = -1000000000.0
LN_EPS = 1e-05
SCALE = 1.0 / float(HEAD_DIM) ** 0.5
TURN = 2 * CH
FIRST = TURN
TURNS = 2
LOOP_END = FIRST + TURN * TURNS
SP_TURNS = 2
OUT_SHARE = [5, 5, 4, 7, 7, 7, 7, 3, 3, 3, 3, 2]
STEPS = UNITS + 2
LAST = BLOCKS - 1


def xattn_kernel(nc, xT, x, mask, ctxT, w0k, w0q, w0v, w1q, w1k, w1v, w1o, cols, rows, out):
    with ExitStack() as ctx:
        def sb(name, shape, dt=F32, stack=ctx):
            return stack.enter_context(nc.sbuf_tensor(name, shape, dt))

        def sem(name):
            return ctx.enter_context(nc.semaphore(name))

        with ExitStack() as prep:
            raw1 = sb("raw1", [P, CH, DIM], F32, prep)
            raw3 = sb("raw3", [P, CH, DIM], F32, prep)
            v1_h = sb("v1_h", [KEYS, BATCH, DIM], F32R, prep)
            ctxT_sb = sb("ctxT_sb", [P, CH, BATCH * KEYS], F32, prep)
            v1T = sb("v1T", [P, CH, BATCH * KEYS], F32, prep)
            rest = sb("rest", [KEYS, BATCH, DIM], F32R, prep)
            v0T = sb("v0T", [P, CH, BATCH * KEYS], F32, prep)
            v0o = sb("v0o", [KEYS, BATCH, DIM], F32, prep)
            k1T = sb("k1T", [P, CH, BATCH * KEYS], F32, prep)
            k0T = sb("k0T", [P, CH, BATCH * KEYS], F32, prep)
            raw0 = sb("raw0", [P, CH, DIM], F32, prep)
            bq0_wide = sb("bq0_wide", [P, CH, P], F32, prep)
            bo_sb = sb("bo_sb", [P, DIM], F32, prep)
            before_y = 4 * CH * BLOCK + 2 * KC * BLOCK + 2 * TILES * GCOLS
            taken = 3 * CH * DIM + 3 * BATCH * DIM + 5 * CH * BATCH * KEYS + CH * P + DIM
            sb("unused", [P, before_y - taken], F32, prep)
            raw2 = sb("raw2", [P, CH, DIM], F32, prep)
        ct_h = sb("ct_h", [P, 2, CH, BLOCK], F32R)
        ct_l = sb("ct_l", [P, 2, CH, BLOCK], F32R)
        pt_h = sb("pt_h", [KROWS, KC, BLOCK], F32R)
        pt_l = sb("pt_l", [KROWS, KC, BLOCK], F32R)
        prob = sb("prob", [P, 2, TILES, GCOLS])
        y = sb("y", [P, TILES, DIM])

        wq_h = sb("wq_h", [P, CH, DIM], F32R)
        wq_l = sb("wq_l", [P, CH, DIM], F32R)
        wo_h = sb("wo_h", [P, CH, DIM], F32R)
        wo_l = sb("wo_l", [P, CH, DIM], F32R)
        a0 = sb("a0", [P, CH, BATCH * KEYS])
        c0 = sb("c0", [P, BATCH * KEYS])
        u_a = sb("u_a", [P, BATCH, DIM], F32R)
        u_b = sb("u_b", [BROWS, BATCH, DIM], F32R)
        v0_a = sb("v0_a", [P, BATCH, DIM], F32R)
        v0_b = sb("v0_b", [BROWS, BATCH, DIM], F32R)
        kd_h = sb("kd_h", [P, BATCH, CH, GCOLS], F32R)
        kd_l = sb("kd_l", [P, BATCH, CH, GCOLS], F32R)
        vd_h = sb("vd_h", [KROWS, BATCH, CH, KC, P], F32R)
        vd_l = sb("vd_l", [KROWS, BATCH, CH, KC, P], F32R)
        cols_sb = sb("cols_sb", [P, 6, CH])
        rows_sb = sb("rows_sb", [P, 2, DIM])
        bk1_scaled = sb("bk1_scaled", [P, CH])
        ident = sb("ident", [P, P])
        minus_half = sb("minus_half", [P, TILES])

        x_raw = sb("x_raw", [P, CH, BLOCK])
        last_y = x_raw
        x_h = sb("x_h", [P, CH, BLOCK], F32R)
        x_l = sb("x_l", [P, CH, BLOCK], F32R)
        mask_sb = sb("mask_sb", [P, TILES, KEYS], I32)
        n0 = sb("n0", [P, TILES, KEYS])
        m0 = sb("m0", [P, TILES, KEYS])
        stat0 = sb("stat0", [P, 3, TILES])
        p0_a = sb("p0_a", [P, 2, BLOCK], F32R)
        p0_b = sb("p0_b", [BROWS, 2, BLOCK], F32R)
        p0_l = sb("p0_l", [KEYS, BLOCK], F32R)
        q_h = sb("q_h", [P, 2, BLOCK], F32R)
        q_l = sb("q_l", [P, 2, BLOCK], F32R)
        mx = sb("mx", [P, 2, TILES, GROUP_HEADS])
        sm = sb("sm", [P, 2, TILES, GROUP_HEADS])
        rc = sb("rc", [P, 2, TILES, GROUP_HEADS])
        bn6 = sb("bn6", [P, TILES, 6])
        both = sb("both", [P, TILES, 3])
        diff = sb("diff", [P, TILES])
        within = sb("within", [P, TILES])
        between = sb("between", [P, TILES])
        ve = sb("ve", [P, TILES])
        rs = sb("rs", [P, TILES])
        nb = sb("nb", [P, TILES])

        bank = [ctx.enter_context(nc.psum_tensor(f"bank{n}", [P, 512], F32)) for n in range(8)]
        last_out = [bank[7], bank[1], bank[2], bank[6]]
        ps_q, ps_s, ps_t, ps_pv, ps_out, ps_0 = bank[0], bank[1:3], bank[3:5], bank[5], bank[6], bank[7]

        ld_ctx, ld_cols, ld_rows = sem("ld_ctx"), sem("ld_cols"), sem("ld_rows")
        ld_w0k, ld_w0q, ld_w0v, ld_w1q = [sem("ld_w0k0"), sem("ld_w0k1")], [sem("ld_w0q0"), sem("ld_w0q1")], sem("ld_w0v"), sem("ld_w1q")
        ld_w1k, ld_w1v, ld_w1o = sem("ld_w1k"), sem("ld_w1v"), sem("ld_w1o")
        ld_xT, ld_mask, ld_bo = sem("ld_xT"), sem("ld_mask"), sem("ld_bo")
        ld_x = [sem(f"ld_x{t}") for t in range(TILES)]
        ld_last = sem("ld_last")
        vd_placed = sem("vd_placed")
        u_stacked, v0_stacked, p0_stacked = [sem("u_stacked0"), sem("u_stacked1")], sem("v0_stacked"), sem("p0_stacked")
        stored = [sem(f"stored{t}") for t in range(TILES)]
        mm_k0T, mm_a0, mm_c0, mm_v0T = sem("mm_k0T"), sem("mm_a0"), sem("mm_c0"), sem("mm_v0T")
        mm_v0, mm_u, mm_k1T, mm_v1T, mm_v1 = sem("mm_v0"), sem("mm_u"), sem("mm_k1T"), sem("mm_v1T"), sem("mm_v1")
        k0T_ready, v0T_ready, k1T_ready, v1T_ready = sem("k0T_ready"), sem("v0T_ready"), sem("k1T_ready"), sem("v1T_ready")
        wq_h_ready, wo_h_ready, u_h_ready, v1_h_ready = sem("wq_h_ready"), sem("wo_h_ready"), sem("u_h_ready"), sem("v1_h_ready")
        bk1_ready = sem("bk1_ready")
        a0_ready, c0_ready, bq0_ready, u_ready, v0o_ready = sem("a0_ready"), sem("c0_ready"), sem("bq0_ready"), sem("u_ready"), sem("v0o_ready")
        v0_h_ready, v0_ready, kd_h_ready, kd_ready = sem("v0_h_ready"), sem("v0_ready"), sem("kd_h_ready"), sem("kd_ready")
        v1_ready, wq_ready, wo_ready = sem("v1_ready"), sem("wq_ready"), sem("wo_ready")
        ident_zero, ident_ready, kd_zero, vd_zero, const_ready = sem("ident_zero"), sem("ident_ready"), sem("kd_zero"), sem("vd_zero"), sem("const_ready")
        q_done, s_done, t_done, pv_done, out_done = sem("q_done"), sem("s_done"), sem("t_done"), sem("pv_done"), sem("out_done")
        l0_done, p0t_done = sem("l0_done"), sem("p0t_done")
        qh_ready, exp_done, pth_ready, cth_ready = sem("qh_ready"), sem("exp_done"), sem("pth_ready"), sem("cth_ready")
        xh_ready, exp0_done, p0h_ready, z_done = sem("xh_ready"), sem("exp0_done"), sem("p0h_ready"), sem("z_done")
        ql_ready, max_done, sum_done, rcp_done = sem("ql_ready"), sem("max_done"), sem("sum_done"), sem("rcp_done")
        ptl_ready, ctl_ready, y_done, bn_done, nb_done = sem("ptl_ready"), sem("ctl_ready"), sem("y_done"), sem("bn_done"), sem("nb_done")
        last_gamma_done, last_beta_done = sem("last_gamma_done"), sem("last_beta_done")
        both_done, diff_done, within_done, between_done, var_done = sem("both_done"), sem("diff_done"), sem("within_done"), sem("between_done"), sem("var_done")
        neg0_done, kept0_done = sem("neg0_done"), sem("kept0_done")
        add0_done, sel0_done, max0_done, sub0_done = sem("add0_done"), sem("sel0_done"), sem("max0_done"), sem("sub0_done")
        sum0_done, rcp0_done, prob0_done, p0l_ready = sem("sum0_done"), sem("rcp0_done"), sem("prob0_done"), sem("p0l_ready")
        prob_done, xl_ready = sem("prob_done"), sem("xl_ready")
        rs_done, gamma_done, beta_done = sem("rs_done"), sem("gamma_done"), sem("beta_done")

        def units(i, k):
            return TURN * i + k

        def tiles(i, k, t):
            return TILES * TURN * i + TILES * k + t

        def chunks(i, k, c):
            return KC * TURN * i + KC * k + c

        def blocks(i, b):
            return 2 * i + b

        def wait(eng, semaphore, count):
            if not (type(count) is int and count <= 0):
                eng.wait_ge(semaphore, count)

        def unit_exists(i, k):
            return type(i) is not int or 0 <= k < UNITS

        def is_last(i, b):
            return type(i) is int and b == LAST

        def block_exists(i, b):
            return type(i) is not int or 0 <= b < BLOCKS

        def run(eng, step):
            for k in range(FIRST):
                step(0, k)
            with eng.Fori(0, TURNS) as i:
                for k in range(FIRST, FIRST + TURN):
                    step(i, k)
            for k in range(LOOP_END, STEPS):
                step(0, k)

        def part3(a_h, a_l, b_h, b_l):
            return ((a_h, b_h), (a_l, b_h), (a_h, b_l))

        def f32(ap):
            return ap.bitcast(F32)

        def wide(ap, n):
            return ap.unsqueeze(2).to_broadcast([ap.shape[0], ap.shape[1], n])

        block = ctx.enter_context(nc.Block())

        @block.sync
        def _(sp):
            sp.dma_start(ctxT_sb[:], ctxT.rearrange("(c p) k -> p c k", p=P)).then_inc(ld_ctx, 16)
            for raw, w, loaded in ((raw0, w0k, ld_w0k), (raw1, w0q, ld_w0q)):
                for h in range(2):
                    own = slice(h * DIM // 2, (h + 1) * DIM // 2)
                    sp.dma_start(raw[:, :, own], w.rearrange("(c p) e -> p c e", p=P)[:, :, own]).then_inc(loaded[h], 16)
            sp.dma_start(x_raw[:].rearrange("p c t -> p (c t)"), xT[0, 0]).then_inc(ld_xT, 16)
            sp.dma_start(raw3[:], w0v.rearrange("(c p) e -> p c e", p=P)).then_inc(ld_w0v, 16)
            sp.dma_start(raw2[:], w1q.rearrange("(c p) e -> p c e", p=P)).then_inc(ld_w1q, 16)
            sp.wait_ge(mm_k0T, 2)
            sp.dma_start(raw0[:], w1k.rearrange("(c p) e -> p c e", p=P)).then_inc(ld_w1k, 16)
            sp.wait_ge(mm_a0, 2)
            sp.dma_start(raw1[:], w1v.rearrange("(c p) e -> p c e", p=P)).then_inc(ld_w1v, 16)
            sp.wait_ge(mm_v0T, 2)
            sp.dma_start(raw3[:], w1o.rearrange("(c p) e -> p c e", p=P)).then_inc(ld_w1o, 16)

            def next_inputs(i, b):
                if not block_exists(i, b + 1):
                    return
                j = i + (b + 1) // 2
                wait(sp, xl_ready, CH * blocks(i, b + 1))
                wait(sp, sel0_done, blocks(i, b + 1))
                sp.dma_start(x_raw[:].rearrange("p c t -> p (c t)"), xT[(b + 1) % 2, j]).then_inc(ld_xT, 16)
                sp.dma_start(mask_sb[:].rearrange("p t k -> p (t k)"), mask[(b + 1) % 2, j]).then_inc(ld_mask, 16)

            def load_rows(i, b, t):
                if not block_exists(i, b) or is_last(i, b):
                    return
                wait(sp, stored[t], 16 * blocks(i, b))
                sp.dma_start(y[:, t, :], x[b % 2, TILES * (i + b // 2) + t]).then_inc(ld_x[t], 16)

            def store(i, b):
                if not block_exists(i, b):
                    return
                for t in range(TILES):
                    wait(sp, beta_done, TILES * blocks(i, b) + t + 1)
                    sp.dma_start(out[b % 2, i + b // 2, t], y[:, t, :]).then_inc(stored[t], 16)
                    if t > 0:
                        load_rows(i, b + 1, t - 1)
                load_rows(i, b + 1, TILES - 1)

            def move(to, frm, done):
                sp.dma_start(f32(to), f32(frm)).then_inc(done, 16)

            def stack_weights(a, b, own, done, rounded, remaining, count):
                sp.wait_ge(rounded, count)
                move(a[KEYS:P, own], a[0:TAIL, own], done)
                move(b[0:REST, own], a[TAIL:KEYS, own], done)
                sp.wait_ge(remaining, count)
                move(b[REST:BROWS, own], rest[:, own], done)

            def stack_probs(i, b):
                if not block_exists(i, b):
                    return
                wait(sp, p0h_ready, blocks(i, b) + 1)
                move(p0_b[REST:BROWS, b % 2], p0_a[0:KEYS, b % 2], p0_stacked)
                wait(sp, p0l_ready, blocks(i, b) + 1)
                move(p0_a[KEYS:P, b % 2], p0_l[0:TAIL], p0_stacked)
                move(p0_b[0:REST, b % 2], p0_l[TAIL:KEYS], p0_stacked)

            next_inputs(0, 0)
            stack_probs(0, 0)
            stack_weights(u_a, u_b, slice(0, 1), u_stacked[0], u_h_ready, u_ready, 1)
            stack_weights(v0_a, v0_b, slice(0, BATCH), v0_stacked, v0_h_ready, v0_ready, BATCH)
            sp.wait_ge(vd_zero, 2)
            for part, blocks_of, ready in ((v1_h, vd_h, v1_h_ready), (rest, vd_l, v1_ready)):
                sp.wait_ge(ready, BATCH)
                for c in range(KC):
                    done = KSTART[c] if c == 0 else KSTART[c - 1] + KROWS
                    while done < KSTART[c] + KROWS:
                        head, key = divmod(done, KEYS)
                        m = min(KEYS - key, KSTART[c] + KROWS - done)
                        r = done - KSTART[c]
                        own = slice(head * HEAD_DIM, (head + 1) * HEAD_DIM)
                        sp.dma_start(
                            f32(blocks_of[r:r + m]).rearrange("r b g c d -> r (b g) c d")[:, :, c, own],
                            f32(part[key:key + m]).rearrange("r b (g d) -> r (b g) d", d=P)[:, :, own],
                        ).then_inc(vd_placed, 16)
                        done += m
            stack_weights(u_a, u_b, slice(1, 2), u_stacked[1], u_h_ready, u_ready, 2)
            sp.wait_ge(mm_u, BATCH)
            sp.wait_ge(wq_ready, CH)
            for t in range(TILES):
                load_rows(0, 0, t)
            stack_probs(0, 1)
            next_inputs(0, 1)
            with sp.Fori(0, SP_TURNS) as i:
                for b in (2, 3):
                    stack_probs(i, b)
                    next_inputs(i, b)
                    store(i, b - 2)
            for b in range(2 + 2 * SP_TURNS, BLOCKS + 1):
                stack_probs(0, b)
                next_inputs(0, b)
                if b == BLOCKS:
                    sp.wait_ge(xl_ready, CH * BLOCKS)
                    sp.wait_ge(xh_ready, CH * BLOCKS)
                    last_x = x[LAST % 2, TILES * (LAST // 2):TILES * (LAST // 2 + 1)]
                    sp.dma_start(last_y[:], last_x.rearrange("t p d -> p t d")).then_inc(ld_last, 16)
                store(0, b - 2)
            for t, (semaphore, count) in enumerate(((beta_done, TILES * LAST + 1), (last_beta_done, 1),
                                                    (last_beta_done, 2), (last_beta_done, 3))):
                sp.wait_ge(semaphore, count)
                sp.dma_start(out[LAST % 2, LAST // 2, t], last_y[:, t, :]).then_inc(stored[t], 16)
            for t in range(TILES):
                sp.wait_ge(stored[t], 16 * BLOCKS)

        @block.gpsimd
        def _(pool):
            def x_rest(i, b, c):
                if not block_exists(i, b):
                    return
                wait(pool, xh_ready, CH * blocks(i, b) + c + 1)
                nc.gpsimd.tensor_tensor(x_l[:, c], x_raw[:, c], f32(x_h[:, c]), ALU.subtract).then_inc(xl_ready, 1)

            nc.gpsimd.memset(ident[:], 0.0).then_inc(ident_zero, 1)
            pool.wait_ge(ident_zero, 1)
            nc.gpsimd.affine_select(out=ident[:], in_=ident[:], compare_op=ALU.not_equal, fill=1.0, base=0,
                                    pattern=[[-1, P]], channel_multiplier=1).then_inc(ident_ready, 1)
            nc.gpsimd.memset(minus_half[:], -0.5).then_inc(const_ready, 1)
            for part in (kd_h, kd_l):
                nc.gpsimd.memset(f32(part[:]), 0.0).then_inc(kd_zero, 1)
            for c in range(CH):
                x_rest(0, 0, c)
            for part in (vd_h, vd_l):
                nc.gpsimd.memset(f32(part[:]), 0.0).then_inc(vd_zero, 1)

            def wo_rest(c):
                pool.wait_ge(wo_h_ready, c + 1)
                nc.gpsimd.tensor_tensor(wo_l[:, c], raw3[:, c], f32(wo_h[:, c]), ALU.subtract).then_inc(wo_ready, 1)

            def scale_probs(i, k, t):
                if not unit_exists(i, k):
                    return
                wait(pool, rcp_done, tiles(i, k, t) + 1)
                ap = prob[:, k % 2, t].rearrange("p (h k) -> p h k", k=KEYS)
                nc.gpsimd.tensor_tensor(ap, ap, wide(rc[:, k % 2, t], KEYS), ALU.mult).then_inc(prob_done, 1)

            def root(i, b, h):
                if not block_exists(i, b):
                    return
                own = slice(2 * h, 2 * h + 2)
                wait(pool, var_done, 2 * blocks(i, b) + h + 1)
                nc.gpsimd.tensor_tensor(rs[:, own], ve[:, own], minus_half[:, own], ALU.pow).then_inc(rs_done, 1)

            def affine(i, b, t):
                if not block_exists(i, b):
                    return
                m = TILES * blocks(i, b) + t
                wait(pool, z_done, m + 1)
                nc.gpsimd.tensor_tensor(y[:, t], y[:, t], rows_sb[:, 0], ALU.mult).then_inc(gamma_done, 1)
                wait(pool, gamma_done, m + 1)
                nc.gpsimd.tensor_tensor(y[:, t], y[:, t], rows_sb[:, 1], ALU.add).then_inc(beta_done, 1)

            def step(i, k):
                g, b = k % CH, k // CH
                scale_probs(i, k - 1, 3)
                if type(i) is int and k == 1:
                    wo_rest(0)
                if g == 3:
                    x_rest(i, b + 1, 2)
                    x_rest(i, b + 1, 3)
                if g == 0:
                    affine(i, b - 2, 0)
                scale_probs(i, k, 0)
                if type(i) is int and k == 1:
                    wo_rest(1)
                if g == 1:
                    affine(i, b - 2, 2)
                scale_probs(i, k, 1)
                if type(i) is int and k == 1:
                    wo_rest(2)
                if g == 3:
                    root(i, b - 1, 0)
                if g == 0:
                    root(i, b - 2, 1)
                    affine(i, b - 2, 1)
                scale_probs(i, k, 2)
                if type(i) is int and k == 1:
                    wo_rest(3)
                if g == 2:
                    x_rest(i, b + 1, 0)
                    x_rest(i, b + 1, 1)
                if g == 1:
                    affine(i, b - 2, 3)

            pool.wait_ge(ld_rows, 16)
            pool.wait_ge(const_ready, 1)
            run(pool, step)
            root(0, LAST, 0)
            root(0, LAST, 1)
            m = TILES * LAST
            pool.wait_ge(z_done, m + 1)
            nc.gpsimd.tensor_tensor(last_y[:, 0], last_y[:, 0], rows_sb[:, 0], ALU.mult).then_inc(gamma_done, 1)
            pool.wait_ge(gamma_done, m + 1)
            nc.gpsimd.tensor_tensor(last_y[:, 0], last_y[:, 0], rows_sb[:, 1], ALU.add).then_inc(beta_done, 1)

        @block.scalar
        def _(act):
            act.dma_start(cols_sb[:].rearrange("p a c -> p (a c)"), cols).then_inc(ld_cols, 16)
            act.dma_start(mask_sb[:].rearrange("p t k -> p (t k)"), mask[0, 0]).then_inc(ld_mask, 16)
            flat = rows.rearrange("(o n) -> o n", o=1)
            act.dma_start(bo_sb[:], flat[:, 2 * DIM:3 * DIM].to_broadcast([P, DIM])).then_inc(ld_bo, 16)
            act.dma_start(rows_sb[:].rearrange("p a d -> p (a d)"),
                          flat[:, 0:2 * DIM].to_broadcast([P, 2 * DIM])).then_inc(ld_rows, 16)

            def leave(banks, made, to, bias, ready, scale=1.0, first=0, last=CH):
                for c in range(first, last):
                    act.wait_ge(made, c // 2 + 1)
                    src = banks[c // 2][:, 0:2 * BATCH * KEYS].rearrange("p (e k) -> p e k", e=2)[:, c % 2]
                    nc.scalar.activation(to[:, c], src, ACT.Identity, bias=bias[:, c:c + 1], scale=scale).then_inc(ready, 1)

            def round_x(i, b, first, last):
                if not block_exists(i, b):
                    return
                wait(act, ld_xT, 16 * (blocks(i, b) + 1))
                wait(act, q_done, CH * blocks(i, b))
                for c in range(first, last):
                    nc.scalar.activation(x_h[:, c], x_raw[:, c], ACT.Copy).then_inc(xh_ready, 1)

            def exp0(i, b):
                if not block_exists(i, b):
                    return
                wait(act, sub0_done, blocks(i, b) + 1)
                nc.scalar.activation(m0[:], m0[:], ACT.Exp).then_inc(exp0_done, 1)

            def round_p0(i, b):
                if not block_exists(i, b):
                    return
                wait(act, p0t_done, blocks(i, b) + 1)
                nc.scalar.activation(p0_a[0:KEYS, b % 2], ps_0[0:KEYS, :], ACT.Copy).then_inc(p0h_ready, 1)

            def round_q(i, k):
                if not unit_exists(i, k):
                    return
                wait(act, q_done, units(i, k) + 1)
                nc.scalar.activation(q_h[:, k % 2], ps_q[:], ACT.Identity,
                                     bias=cols_sb[:, 3, k % CH:k % CH + 1]).then_inc(qh_ready, 1)

            act.wait_ge(ld_cols, 16)
            leave(bank[1:3], mm_k0T, k0T, cols_sb[:, 1], k0T_ready)
            round_x(0, 0, 0, CH)
            leave(bank[5:7], mm_v0T, v0T, cols_sb[:, 2], v0T_ready)
            exp0(0, 0)
            act.wait_ge(ld_w1q, 16)
            for c in range(CH):
                nc.scalar.activation(wq_h[:, c], raw2[:, c], ACT.Copy).then_inc(wq_h_ready, 1)
            act.wait_ge(bk1_ready, 1)
            leave(bank[1:3], mm_k1T, k1T, bk1_scaled, k1T_ready, scale=SCALE)
            round_p0(0, 0)

            def round_u(b):
                act.wait_ge(mm_u, b + 1)
                nc.scalar.activation(u_a[0:KEYS, b], bank[5 + b][0:KEYS, :], ACT.Copy).then_inc(u_h_ready, 1)

            round_u(0)
            leave(bank[5:7], mm_v1T, v1T, cols_sb[:, 5], v1T_ready, first=0, last=2)
            round_q(0, 0)
            leave(bank[5:7], mm_v1T, v1T, cols_sb[:, 5], v1T_ready, first=2, last=CH)

            def exps(i, k, t):
                if not unit_exists(i, k):
                    return
                wait(act, max_done, tiles(i, k, t) + 1)
                for h in range(GROUP_HEADS):
                    own = slice(h * KEYS, (h + 1) * KEYS)
                    e = nc.scalar.activation(prob[:, k % 2, t, own], ps_s[t % 2][:, own], ACT.Exp, bias=mx[:, k % 2, t, h:h + 1])
                e.then_inc(exp_done, 1)

            def round_pt(i, k, c):
                if not unit_exists(i, k):
                    return
                wait(act, t_done, chunks(i, k, c) + 1)
                nc.scalar.activation(pt_h[:, c], ps_t[c % 2][0:KROWS, :], ACT.Copy).then_inc(pth_ready, 1)

            def round_ct(i, k):
                if not unit_exists(i, k):
                    return
                wait(act, pv_done, units(i, k) + 1)
                nc.scalar.activation(ct_h[:, k // CH % 2, k % CH], ps_pv[:], ACT.Copy).then_inc(cth_ready, 1)

            def normalise(i, b, t):
                if not block_exists(i, b):
                    return
                wait(act, nb_done, 2 * blocks(i, b) + t // 2 + 1)
                rows_of = (last_y if is_last(i, b) else y)[:, t]
                nc.scalar.activation(rows_of, rows_of, ACT.Identity, bias=nb[:, t:t + 1],
                                     scale=rs[:, t:t + 1]).then_inc(z_done, 1)

            def step(i, k):
                g, b = k % CH, k // CH
                round_pt(i, k - 2, 2)
                if g == 3:
                    round_p0(i, b + 1)
                exps(i, k, 0)
                if g == 0:
                    normalise(i, b - 2, 1)
                if g == 1:
                    normalise(i, b - 2, 2)
                exps(i, k, 1)
                round_ct(i, k - 2)
                if g == 1:
                    normalise(i, b - 2, 3)
                    exp0(i, b + 1)
                round_pt(i, k - 1, 0)
                if type(i) is int and k == 0:
                    for v in range(BATCH):
                        act.wait_ge(mm_v1, v + 1)
                        nc.scalar.activation(v1_h[:, v], bank[5 + v][0:KEYS, :], ACT.Copy).then_inc(v1_h_ready, 1)
                exps(i, k, 2)
                if type(i) is int and k == 1:
                    round_u(1)
                round_q(i, k + 1)
                round_pt(i, k - 1, 1)
                if g == 2:
                    round_x(i, b + 1, 0, 2)
                exps(i, k, 3)
                if type(i) is int and k == 0:
                    act.wait_ge(ld_w1o, 16)
                    for c in range(CH):
                        nc.scalar.activation(wo_h[:, c], raw3[:, c], ACT.Copy).then_inc(wo_h_ready, 1)
                if g == 2:
                    round_x(i, b + 1, 2, CH)
                if g == 3:
                    normalise(i, b - 1, 0)

            run(act, step)
            for t in range(TILES):
                normalise(0, LAST, t)

        @block.vector
        def _(dve):
            def layer0_scores(i, b):
                if not block_exists(i, b):
                    return
                n = blocks(i, b)
                v = slice(b % 2 * KEYS, (b % 2 + 1) * KEYS)
                wait(dve, l0_done, n + 1)
                nc.vector.tensor_tensor(m0[:], ps_0[:, 0:TILES * KEYS].rearrange("p (t k) -> p t k", k=KEYS),
                                        c0[:, v].unsqueeze(1).to_broadcast([P, TILES, KEYS]), ALU.add).then_inc(add0_done, 1)
                wait(dve, ld_mask, 16 * (n + 1))
                nc.vector.tensor_scalar(n0[:], mask_sb[:], 0.0, NEG, ALU.is_equal, ALU.mult).then_inc(neg0_done, 1)
                wait(dve, add0_done, n + 1)
                wait(dve, neg0_done, n + 1)
                nc.vector.scalar_tensor_tensor(out=m0[:], in0=n0[:], scalar=0.0, in1=m0[:],
                                               op0=ALU.is_equal, op1=ALU.mult).then_inc(kept0_done, 1)
                wait(dve, kept0_done, n + 1)
                nc.vector.tensor_tensor(m0[:], m0[:], n0[:], ALU.add).then_inc(sel0_done, 1)

            def layer0_shift(i, b):
                if not block_exists(i, b):
                    return
                n = blocks(i, b)
                wait(dve, sel0_done, n + 1)
                nc.vector.reduce_max(stat0[:, 0], m0[:], AX_X).then_inc(max0_done, 1)
                wait(dve, max0_done, n + 1)
                nc.vector.tensor_tensor(m0[:], m0[:], wide(stat0[:, 0], KEYS), ALU.subtract).then_inc(sub0_done, 1)

            def layer0_probs(i, b):
                if not block_exists(i, b):
                    return
                n = blocks(i, b)
                wait(dve, exp0_done, n + 1)
                nc.vector.reduce_sum(stat0[:, 1], m0[:], AX_X).then_inc(sum0_done, 1)
                wait(dve, sum0_done, n + 1)
                nc.vector.reciprocal(stat0[:, 2], stat0[:, 1]).then_inc(rcp0_done, 1)
                wait(dve, rcp0_done, n + 1)
                nc.vector.tensor_tensor(m0[:], m0[:], wide(stat0[:, 2], KEYS), ALU.mult).then_inc(prob0_done, 1)

            def p0_rest(i, b):
                if not block_exists(i, b):
                    return
                wait(dve, p0h_ready, blocks(i, b) + 1)
                nc.vector.tensor_tensor(p0_l[:], ps_0[0:KEYS, :], f32(p0_a[0:KEYS, b % 2]),
                                        ALU.subtract).then_inc(p0l_ready, 1)

            def q_rest(i, k):
                if not unit_exists(i, k):
                    return
                wait(dve, qh_ready, units(i, k) + 1)
                nc.vector.scalar_tensor_tensor(out=q_l[:, k % 2], in0=ps_q[:], scalar=cols_sb[:, 3, k % CH:k % CH + 1],
                                               in1=f32(q_h[:, k % 2]), op0=ALU.add, op1=ALU.subtract).then_inc(ql_ready, 1)

            dve.wait_ge(ld_cols, 16)
            nc.vector.tensor_copy(bq0_wide[:], wide(cols_sb[:, 0], P)).then_inc(bq0_ready, 1)
            nc.vector.tensor_scalar(bk1_scaled[:], cols_sb[:, 4], SCALE, None, ALU.mult).then_inc(bk1_ready, 1)
            for h in range(2):
                dve.wait_ge(mm_a0, h + 1)
                nc.vector.tensor_copy(a0[:, 2 * h:2 * h + 2].rearrange("p c k -> p (c k)"),
                                      bank[3 + h][:, 0:2 * BATCH * KEYS]).then_inc(a0_ready, 1)
            dve.wait_ge(mm_c0, 1)
            nc.vector.tensor_copy(c0[:], ps_0[:, 0:BATCH * KEYS]).then_inc(c0_ready, 1)
            dve.wait_ge(c0_ready, 1)
            layer0_scores(0, 0)
            layer0_shift(0, 0)
            layer0_probs(0, 0)
            for c in range(CH):
                dve.wait_ge(wq_h_ready, c + 1)
                nc.vector.tensor_tensor(wq_l[:, c], raw2[:, c], f32(wq_h[:, c]), ALU.subtract).then_inc(wq_ready, 1)
            dve.wait_ge(kd_zero, 2)
            dve.wait_ge(k1T_ready, CH)

            def spread_keys(b):
                at = [(slice(h * HEAD_DIM, (h + 1) * HEAD_DIM), slice(h * KEYS, (h + 1) * KEYS)) for h in range(GROUP_HEADS)]
                own = slice(b * KEYS, (b + 1) * KEYS)
                for rows_of, cols_of in at:
                    nc.vector.tensor_copy(kd_h[rows_of, b, :, cols_of], k1T[rows_of, :, own]).then_inc(kd_h_ready, 1)
                for h, (rows_of, cols_of) in enumerate(at):
                    dve.wait_ge(kd_h_ready, GROUP_HEADS * b + h + 1)
                    nc.vector.tensor_tensor(kd_l[rows_of, b, :, cols_of], k1T[rows_of, :, own],
                                            f32(kd_h[rows_of, b, :, cols_of]), ALU.subtract).then_inc(kd_ready, 1)


            def u_rest(b):
                dve.wait_ge(u_h_ready, b + 1)
                if b == 1:
                    dve.wait_ge(vd_placed, 16 * 12)
                nc.vector.tensor_tensor(rest[:, b], bank[5 + b][0:KEYS, :], f32(u_a[0:KEYS, b]), ALU.subtract).then_inc(u_ready, 1)

            p0_rest(0, 0)
            u_rest(0)
            spread_keys(0)
            dve.wait_ge(ld_bo, 16)
            for b in range(BATCH):
                dve.wait_ge(mm_v0, b + 1)
                nc.vector.tensor_tensor(v0o[:, b], bank[3 + b][0:KEYS, :], bo_sb[0:KEYS], ALU.add).then_inc(v0o_ready, 1)
            for v in range(BATCH):
                dve.wait_ge(v0o_ready, v + 1)
                nc.vector.tensor_copy(v0_a[0:KEYS, v], v0o[:, v]).then_inc(v0_h_ready, 1)
            q_rest(0, 0)
            for v in range(BATCH):
                dve.wait_ge(v0_h_ready, v + 1)
                dve.wait_ge(u_stacked[0], 48)
                nc.vector.tensor_tensor(rest[:, v], v0o[:, v], f32(v0_a[0:KEYS, v]), ALU.subtract).then_inc(v0_ready, 1)

            def largest(i, k, t):
                if not unit_exists(i, k):
                    return
                wait(dve, s_done, tiles(i, k, t) + 1)
                nc.vector.reduce_max(mx[:, k % 2, t], ps_s[t % 2][:, 0:GCOLS].rearrange("p (h k) -> p h k", k=KEYS),
                                     AX_X, negate=True).then_inc(max_done, 1)

            def inverse_sums(i, k, t):
                if not unit_exists(i, k):
                    return
                wait(dve, exp_done, tiles(i, k, t) + 1)
                nc.vector.reduce_sum(sm[:, k % 2, t], prob[:, k % 2, t].rearrange("p (h k) -> p h k", k=KEYS),
                                     AX_X).then_inc(sum_done, 1)
                wait(dve, sum_done, tiles(i, k, t) + 1)
                nc.vector.reciprocal(rc[:, k % 2, t], sm[:, k % 2, t]).then_inc(rcp_done, 1)

            def pt_rest(i, k, c):
                if not unit_exists(i, k):
                    return
                wait(dve, pth_ready, chunks(i, k, c) + 1)
                nc.vector.tensor_tensor(pt_l[:, c], ps_t[c % 2][0:KROWS, :], f32(pt_h[:, c]),
                                        ALU.subtract).then_inc(ptl_ready, 1)

            def ct_rest(i, k):
                if not unit_exists(i, k):
                    return
                wait(dve, cth_ready, units(i, k) + 1)
                nc.vector.tensor_tensor(ct_l[:, k // CH % 2, k % CH], ps_pv[:], f32(ct_h[:, k // CH % 2, k % CH]),
                                        ALU.subtract).then_inc(ctl_ready, 1)

            def residual(i, b, t):
                if not block_exists(i, b):
                    return
                m = TILES * blocks(i, b) + t
                wait(dve, out_done, m + 1)
                if is_last(i, b):
                    dve.wait_ge(ld_last, 16)
                else:
                    wait(dve, ld_x[t], 16 * (blocks(i, b) + 1))
                ps, rows_of = (last_out[t], last_y[:, t]) if is_last(i, b) else (ps_out, y[:, t])
                nc.vector.tensor_tensor(rows_of, ps[:], rows_of, ALU.add).then_inc(y_done, 1)

            def statistics(i, b, t):
                if not block_exists(i, b):
                    return
                m = TILES * blocks(i, b) + t
                wait(dve, y_done, m + 1)
                nc.vector.bn_stats(bn6[:, t], (last_y if is_last(i, b) else y)[:, t]).then_inc(bn_done, 1)

            def variance(i, b, h):
                if not block_exists(i, b):
                    return
                n, own = 2 * blocks(i, b) + h, slice(2 * h, 2 * h + 2)
                wait(dve, bn_done, 2 * (n + 1))
                nc.vector.tensor_tensor(both[:, own], bn6[:, own, 0:3], bn6[:, own, 3:6], ALU.add).then_inc(both_done, 1)
                nc.vector.tensor_tensor(diff[:, own], bn6[:, own, 1], bn6[:, own, 4], ALU.subtract).then_inc(diff_done, 1)
                wait(dve, both_done, n + 1)
                nc.vector.tensor_scalar(within[:, own], both[:, own, 2], 1.0 / DIM, LN_EPS,
                                        ALU.mult, ALU.add).then_inc(within_done, 1)
                wait(dve, diff_done, n + 1)
                nc.vector.scalar_tensor_tensor(out=between[:, own], in0=diff[:, own], scalar=0.25, in1=diff[:, own],
                                               op0=ALU.mult, op1=ALU.mult).then_inc(between_done, 1)
                wait(dve, within_done, n + 1)
                wait(dve, between_done, n + 1)
                nc.vector.tensor_tensor(ve[:, own], within[:, own], between[:, own], ALU.add).then_inc(var_done, 1)

            def offset(i, b, h):
                if not block_exists(i, b):
                    return
                own = slice(2 * h, 2 * h + 2)
                wait(dve, rs_done, 2 * blocks(i, b) + h + 1)
                nc.vector.scalar_tensor_tensor(out=nb[:, own], in0=both[:, own, 1], scalar=-0.5, in1=rs[:, own],
                                               op0=ALU.mult, op1=ALU.mult).then_inc(nb_done, 1)

            def step(i, k):
                g, b = k % CH, k // CH
                largest(i, k, 0)
                if type(i) is int and k == 0:
                    spread_keys(1)
                inverse_sums(i, k - 1, 3)
                pt_rest(i, k - 2, 2)
                if g == 2:
                    layer0_probs(i, b + 1)
                if g == 3:
                    p0_rest(i, b + 1)
                if g == 0:
                    residual(i, b - 2, 3)
                    statistics(i, b - 2, 3)
                if g == 1:
                    layer0_scores(i, b + 1)
                largest(i, k, 1)
                if g == 2:
                    residual(i, b - 1, 1)
                inverse_sums(i, k, 0)
                if g == 0:
                    variance(i, b - 2, 1)
                if g == 1:
                    layer0_shift(i, b + 1)
                if g == 2:
                    statistics(i, b - 1, 1)
                ct_rest(i, k - 2)
                largest(i, k, 2)
                inverse_sums(i, k, 1)
                if type(i) is int and k == 0:
                    for v in range(BATCH):
                        dve.wait_ge(v1_h_ready, v + 1)
                        dve.wait_ge(v0_stacked, 48)
                        nc.vector.tensor_tensor(rest[:, v], bank[5 + v][0:KEYS, :], f32(v1_h[:, v]), ALU.subtract).then_inc(v1_ready, 1)
                pt_rest(i, k - 1, 0)
                if g == 2:
                    variance(i, b - 1, 0)
                if g == 3:
                    offset(i, b - 1, 0)
                if g == 1 and b <= LAST:
                    residual(i, b - 1, 0)
                if g == 2:
                    residual(i, b - 1, 2)
                q_rest(i, k + 1)
                largest(i, k, 3)
                if type(i) is int and k == 1:
                    u_rest(1)
                inverse_sums(i, k, 2)
                pt_rest(i, k - 1, 1)
                if g == 0:
                    offset(i, b - 2, 1)
                if g == 1 and b <= LAST:
                    statistics(i, b - 1, 0)
                if g == 2:
                    statistics(i, b - 1, 2)

            def last_affine(t, n):
                dve.wait_ge(z_done, TILES * LAST + t + 1)
                nc.vector.tensor_tensor(last_y[:, t], last_y[:, t], rows_sb[:, 0], ALU.mult).then_inc(last_gamma_done, 1)
                dve.wait_ge(last_gamma_done, n + 1)
                nc.vector.tensor_tensor(last_y[:, t], last_y[:, t], rows_sb[:, 1], ALU.add).then_inc(last_beta_done, 1)

            run(dve, step)
            residual(0, LAST, 0)
            residual(0, LAST, 1)
            statistics(0, LAST, 0)
            statistics(0, LAST, 1)
            variance(0, LAST, 0)
            residual(0, LAST, 2)
            residual(0, LAST, 3)
            statistics(0, LAST, 2)
            offset(0, LAST, 0)
            statistics(0, LAST, 3)
            variance(0, LAST, 1)
            offset(0, LAST, 1)
            last_affine(1, 0)
            last_affine(2, 1)
            last_affine(3, 2)

        @block.tensor
        def _(pe):
            def project(banks, weights, moving, made, loaded, first=0, last=CH):
                for e in range(first, last):
                    if e % 2 == 0:
                        pe.wait_ge(loaded[e // 2], 16)
                    for c in range(CH):
                        mm = nc.tensor.matmul(banks[e // 2][:, (e % 2) * BATCH * KEYS:(e % 2 + 1) * BATCH * KEYS],
                                              weights[:, c, e * P:(e + 1) * P], moving[:, c],
                                              start=(c == 0), stop=(c == CH - 1))
                    if e % 2:
                        mm.then_inc(made, 1)

            def to_rows(banks, src, made):
                for b in range(BATCH):
                    for e in range(CH):
                        mm = nc.tensor.transpose(banks[b][0:KEYS, e * P:(e + 1) * P],
                                                 src[:, e, b * KEYS:(b + 1) * KEYS], ident[:])
                    mm.then_inc(made, 1)

            def layer0(i, b, t):
                if not block_exists(i, b):
                    return
                if t == 0:
                    wait(pe, ld_xT, 16 * (blocks(i, b) + 1))
                    wait(pe, p0l_ready, blocks(i, b))
                for c in range(CH):
                    mm = nc.tensor.matmul(ps_0[:, t * KEYS:(t + 1) * KEYS], x_raw[:, c, t * P:(t + 1) * P],
                                          a0[:, c, b % 2 * KEYS:(b % 2 + 1) * KEYS],
                                          start=(c == 0), stop=(c == CH - 1))
                if t == TILES - 1:
                    mm.then_inc(l0_done, 1)

            def transpose0(i, b):
                if not block_exists(i, b):
                    return
                wait(pe, prob0_done, blocks(i, b) + 1)
                for t in range(TILES):
                    mm = nc.tensor.transpose(ps_0[0:KEYS, t * P:(t + 1) * P], m0[:, t], ident[:])
                mm.then_inc(p0t_done, 1)

            def query(i, k, first, last):
                if not unit_exists(i, k):
                    return
                b, g = k // CH, k % CH
                own = slice(g * P, (g + 1) * P)
                if first == 0:
                    wait(pe, ql_ready, units(i, k))
                for m in range(first, last):
                    if m < 2 * CH:
                        c = m // 2
                        if g == 0 and m % 2 == 0:
                            wait(pe, xh_ready, CH * blocks(i, b) + c + 1)
                        w, v = (wq_h, wq_l)[m % 2][:, c, own], x_h[:, c]
                    elif m < 3 * CH:
                        c = m - 2 * CH
                        if g == 0:
                            wait(pe, xl_ready, CH * blocks(i, b) + c + 1)
                        w, v = wq_h[:, c, own], x_l[:, c]
                    else:
                        if g == 0 and m == 3 * CH:
                            wait(pe, p0_stacked, 48 * (blocks(i, b) + 1))
                        w, v = ((u_a[:, b % 2, own], p0_a[:, b % 2]), (u_b[:, b % 2, own], p0_b[:, b % 2]))[m - 3 * CH]
                    mm = nc.tensor.matmul(ps_q[:], w, v, start=(m == 0), stop=(m == QUERY - 1))
                if last == QUERY:
                    mm.then_inc(q_done, 1)

            def scores(i, k, t):
                if not unit_exists(i, k):
                    return
                b, g = k // CH, k % CH
                if t == 0:
                    wait(pe, ql_ready, units(i, k) + 1)
                wait(pe, exp_done, tiles(i, k, t) - 1)
                own = slice(t * P, (t + 1) * P)
                for m, (w, v) in enumerate(part3(q_h[:, k % 2, own], q_l[:, k % 2, own], kd_h[:, b % 2, g], kd_l[:, b % 2, g])):
                    mm = nc.tensor.matmul(ps_s[t % 2][:, 0:GCOLS], w, v, start=(m == 0), stop=(m == 2))
                mm.then_inc(s_done, 1)

            def transposes(i, k, c):
                if not unit_exists(i, k):
                    return
                if c == 0:
                    wait(pe, prob_done, tiles(i, k, TILES))
                wait(pe, ptl_ready, chunks(i, k, c) - (0, 2, 1)[c])
                for t in range(TILES):
                    mm = nc.tensor.transpose(ps_t[c % 2][0:KROWS, t * P:(t + 1) * P],
                                             prob[:, k % 2, t, KSTART[c]:KSTART[c] + KROWS], ident[:])
                mm.then_inc(t_done, 1)

            def context(i, k, c):
                if not unit_exists(i, k):
                    return
                b, g = k // CH, k % CH
                if c == 0:
                    wait(pe, ctl_ready, units(i, k))
                wait(pe, ptl_ready, chunks(i, k, c) + 1)
                for m, (w, v) in enumerate(part3(vd_h[:, b % 2, g, c], vd_l[:, b % 2, g, c], pt_h[:, c], pt_l[:, c])):
                    mm = nc.tensor.matmul(ps_pv[:], w, v, start=(c == 0 and m == 0), stop=(c == KC - 1 and m == 2))
                if c == KC - 1:
                    mm.then_inc(pv_done, 1)

            def stacked_values(b, own):
                return (p0_a[:, b % 2, own], v0_a[:, b % 2]), (p0_b[:, b % 2, own], v0_b[:, b % 2])

            def output(i, b, first, last):
                if not block_exists(i, b):
                    return
                for n in range(first, last):
                    t, m = divmod(n, OUTPUT)
                    own = slice(t * P, (t + 1) * P)
                    if m == 0:
                        wait(pe, y_done, TILES * blocks(i, b) + t)
                    if m < 2:
                        w, v = stacked_values(b, own)[m]
                    else:
                        c = (m - 2) // 3
                        if t == 0 and c == CH - 1:
                            wait(pe, ctl_ready, CH * (blocks(i, b) + 1))
                        w, v = part3(ct_h[:, b % 2, c, own], ct_l[:, b % 2, c, own], wo_h[:, c], wo_l[:, c])[(m - 2) % 3]
                    mm = nc.tensor.matmul(ps_out[:], w, v, start=(m == 0), stop=(m == OUTPUT - 1))
                    if m == OUTPUT - 1:
                        mm.then_inc(out_done, 1)

            def last_output(first, last, tiles_of=range(TILES)):
                wait(pe, ctl_ready, CH * LAST + last)
                for t in tiles_of:
                    own = slice(t * P, (t + 1) * P)
                    if first == 0:
                        if last_out[t] is ps_out:
                            wait(pe, y_done, TILES * LAST)
                        for m, (w, v) in enumerate(stacked_values(LAST, own)):
                            nc.tensor.matmul(last_out[t][:], w, v, start=(m == 0), stop=False)
                    for c in range(first, last):
                        for m, (w, v) in enumerate(part3(ct_h[:, LAST % 2, c, own], ct_l[:, LAST % 2, c, own], wo_h[:, c], wo_l[:, c])):
                            mm = nc.tensor.matmul(last_out[t][:], w, v, start=False, stop=(c == CH - 1 and m == 2))
                    if last == CH:
                        mm.then_inc(out_done, 1)

            pe.wait_ge(ld_ctx, 16)
            project(bank[1:3], raw0, ctxT_sb, mm_k0T, ld_w0k)
            pe.wait_ge(k0T_ready, CH)
            project(bank[3:5], raw1, k0T, mm_a0, ld_w0q)
            pe.wait_ge(bq0_ready, 1)
            for c in range(CH):
                mm = nc.tensor.matmul(ps_0[:, 0:BATCH * KEYS], bq0_wide[:, c], k0T[:, c], start=(c == 0), stop=(c == CH - 1))
            mm.then_inc(mm_c0, 1)
            project(bank[5:7], raw3, ctxT_sb, mm_v0T, [ld_w0v, ld_w0v])
            pe.wait_ge(a0_ready, 2)
            pe.wait_ge(c0_ready, 1)
            for t in range(TILES):
                layer0(0, 0, t)
            project(bank[1:3], raw0, ctxT_sb, mm_k1T, [ld_w1k, ld_w1k])
            pe.wait_ge(v0T_ready, CH)
            pe.wait_ge(ident_ready, 1)
            to_rows(bank[3:5], v0T, mm_v0)
            pe.wait_ge(ld_w1q, 16)

            def fold(b, first, last):
                for c in range(first, last):
                    mm = nc.tensor.matmul(bank[5 + b][0:KEYS, :], v0T[:, c, b * KEYS:(b + 1) * KEYS], raw2[:, c],
                                          start=(c == 0), stop=(c == CH - 1))
                if last == CH:
                    mm.then_inc(mm_u, 1)

            transpose0(0, 0)
            fold(0, 0, CH)
            pe.wait_ge(wq_ready, CH)
            query(0, 0, 0, 3 * CH)
            pe.wait_ge(u_ready, 1)
            project(bank[5:7], raw1, ctxT_sb, mm_v1T, [ld_w1v, ld_w1v], 0, 2)
            pe.wait_ge(u_stacked[0], 48)
            query(0, 0, 3 * CH, QUERY)
            project(bank[5:7], raw1, ctxT_sb, mm_v1T, [ld_w1v, ld_w1v], 2, CH)
            pe.wait_ge(kd_ready, GROUP_HEADS)

            def step(i, k):
                g, b = k % CH, k // CH

                def part(t):
                    if type(i) is int and b == LAST + 1:
                        if g == 0 and t < TILES - 1:
                            last_output(0, 2, [t + 1])
                        elif g == 1 and t == 1:
                            last_output(2, 3)
                    elif g == 0:
                        layer0(i, b + 1, t)
                    else:
                        s = TILES * (g - 1) + t
                        output(i, b - 1, sum(OUT_SHARE[:s]), sum(OUT_SHARE[:s + 1]))
                        if is_last(i, b) and g == CH - 1 and t in (0, 2):
                            last_output(t // 2, t // 2 + 1, [0])

                if type(i) is int and k == CH - 1:
                    pe.wait_ge(u_stacked[1], 48)
                if type(i) is int and k == CH:
                    pe.wait_ge(kd_ready, BATCH * GROUP_HEADS)
                if type(i) is int and k == CH + 1:
                    pe.wait_ge(v0_stacked, 48)
                    pe.wait_ge(wo_ready, CH)
                scores(i, k, 0)
                if type(i) is int and k == 1:
                    pe.wait_ge(v1_ready, BATCH)
                    fold(1, 0, 2)
                query(i, k + 1, 0, 5)
                context(i, k - 2, 1)
                part(0)
                scores(i, k, 1)
                context(i, k - 2, 2)
                query(i, k + 1, 5, 10)
                transposes(i, k - 1, 0)
                if type(i) is int and k == 0:
                    pe.wait_ge(v1T_ready, CH)
                    to_rows(bank[5:7], v1T, mm_v1)
                if type(i) is int and k == 1:
                    fold(1, 2, CH)
                part(1)
                scores(i, k, 2)
                query(i, k + 1, 10, QUERY)
                transposes(i, k - 1, 1)
                part(2)
                scores(i, k, 3)
                transposes(i, k - 1, 2)
                if type(i) is int and k == 1:
                    pe.wait_ge(vd_placed, 16 * 12)
                context(i, k - 1, 0)
                part(3)
                if g == 2:
                    transpose0(i, b + 1)

            run(pe, step)
            last_output(3, CH)


def kernel(**inputs):
    import numpy as np
    import concourse.bacc as bacc
    from concourse.bass_utils import run_bass_kernel_spmd

    def arr(name):
        return np.asarray(inputs[name])

    x, ctx, mask = arr("x"), arr("ctx_1024"), arr("mask_BxSxS2_ik0")
    w_qkv, b_qkv = arr("L1_xattn_W_qkv"), arr("L1_xattn_b_qkv")
    nj = SEQ // BLOCK
    by_channel = [arr("L0_xattn_bq"), arr("L0_xattn_bk"), arr("L0_xattn_bv"), b_qkv[:DIM], b_qkv[DIM:2 * DIM], b_qkv[2 * DIM:]]
    arrays = {
        "xT": x.reshape(BATCH, nj, BLOCK, CH, P).transpose(0, 1, 4, 3, 2).reshape(BATCH, nj, P, CH * BLOCK),
        "x": x,
        "mask": mask.reshape(BATCH, nj, TILES, P, KEYS).transpose(0, 1, 3, 2, 4).reshape(BATCH, nj, P, TILES * KEYS),
        "ctxT": ctx.reshape(BATCH * KEYS, DIM).T,
        "w0k": arr("L0_xattn_Wk").T, "w0q": arr("L0_xattn_Wq"), "w0v": arr("L0_xattn_Wv").T,
        "w1q": w_qkv[:DIM].T, "w1k": w_qkv[DIM:2 * DIM].T, "w1v": w_qkv[2 * DIM:].T, "w1o": arr("L1_xattn_W_o").T,
        "cols": np.stack(by_channel).reshape(6, CH, P).transpose(2, 0, 1).reshape(P, 6 * CH),
        "rows": np.concatenate([arr("L1_xattn_ln_gamma"), arr("L1_xattn_ln_beta"), arr("L1_xattn_b_o")]),
    }
    arrays = {"in_" + n: np.ascontiguousarray(a) for n, a in arrays.items()}
    nc = bacc.Bacc("TRN2", target_bir_lowering=False, num_devices=1)
    aps = {n[3:]: nc.dram_tensor(n, a.shape, mybir.dt.from_np(a.dtype), kind="ExternalInput").ap() for n, a in arrays.items()}
    out = nc.dram_tensor("out_0", (BATCH, SEQ, DIM), F32, kind="ExternalOutput").ap()
    aps["x"] = aps["x"].rearrange("b (n p) d -> b n p d", p=P)
    xattn_kernel(nc, **aps, out=out.rearrange("b (j t p) d -> b j t p d", t=TILES, p=P))
    r = run_bass_kernel_spmd(nc, [arrays], core_ids=[0])
    return r.results[0]["out_0"]
```
